# Optimizing a Trainium2 kernel written in Bass

```python
import numpy as np
import jax
import jax.numpy as jnp

def _softmax(x, axis=-1):
    return jax.nn.softmax(x, axis=axis)

def _gelu(x):
    return jax.nn.gelu(x, approximate=True)

def _silu(x):
    return jax.nn.silu(x)

def _sigmoid(x):
    return jax.nn.sigmoid(x)

def _layernorm(x, axis=-1, eps=1e-05):
    m = jnp.mean(x, axis=axis, keepdims=True)
    v = jnp.var(x, axis=axis, keepdims=True)
    return (x - m) / jnp.sqrt(v + eps)

def _scatter_add(tgt, idx, src, axis=0):
    return tgt.at[idx].add(src)

def _segment_sum(src, seg, n):
    return jax.ops.segment_sum(src, seg, n)
kernel_name = 'mk_prb_d1_jaxref_r8_7e4c6c'

def setup_inputs(seed: int=0):
    np.random.seed(seed)
    _w = jnp.asarray

    def _L0_attn_setup():
        import jax, jax.numpy as jnp
        import numpy as np
        D = 128
        H = 16
        DH = 64
        K = 4
        C = H * DH

        def _causal_conv(x, w, b):
            y = jax.lax.conv_general_dilated(x, w, window_strides=(1,), padding=[(K - 1, 0)], feature_group_count=C, dimension_numbers=('NCH', 'OIH', 'NCH'))
            return y + b[None, :, None]
        key = jax.random.key(seed)
        ks = jax.random.split(key, 16)
        s = 0.02
        w = lambda k, shape: jax.random.normal(k, shape, jnp.float32) * s
        return {'hidden_states': jax.random.normal(ks[0], (4, 256, D), jnp.float32), 'Wq': w(ks[1], (C, D)), 'Wk': w(ks[2], (C, D)), 'Wv': w(ks[3], (C, D)), 'Wa': w(ks[4], (H, D)), 'ba': jnp.zeros((H,), jnp.float32), 'Wb': w(ks[5], (H, D)), 'bb': jnp.zeros((H,), jnp.float32), 'conv_q_w': w(ks[6], (C, 1, K)), 'conv_q_b': jnp.zeros((C,), jnp.float32), 'conv_k_w': w(ks[7], (C, 1, K)), 'conv_k_b': jnp.zeros((C,), jnp.float32), 'conv_v_w': w(ks[8], (C, 1, K)), 'conv_v_b': jnp.zeros((C,), jnp.float32), 'Wg': w(ks[9], (C, D)), 'bg': jnp.zeros((C,), jnp.float32), 'Wo': w(ks[10], (D, C))}
    _L0_attn_in = _L0_attn_setup()

    def _L0_ffn_setup():
        import jax, jax.numpy as jnp
        import numpy as np
        D_MODEL = 128
        FF = 512
        E = 8
        TOP_K = 2
        CAP_FACTOR = 1.25
        B, T = (4, 256)

        def _moe_forward(x, gate_w, gate_b, w1, b1, w2, b2):
            Bb, Tt, d = x.shape
            S = Bb * Tt
            C = int(CAP_FACTOR * S / E)
            xf = x.reshape(S, d)
            logits = xf @ gate_w + gate_b
            probs = jax.nn.softmax(logits, axis=1)
            topk_p, topk_i = jax.lax.top_k(probs, TOP_K)
            topk_pn = topk_p / jnp.sum(topk_p, axis=1, keepdims=True)
            rows = jnp.arange(S)
            w_te = jnp.zeros((S, E), xf.dtype).at[rows[:, None], topk_i].set(topk_pn)
            mask = jnp.zeros((S, E), bool).at[rows[:, None], topk_i].set(True)
            rank = jnp.cumsum(mask.astype(jnp.int32), axis=0)
            slot = jnp.where(mask & (rank <= C), rank - 1, C)
            e_grid = jnp.broadcast_to(jnp.arange(E), (S, E))
            t_grid = jnp.broadcast_to(rows[:, None], (S, E))
            buf = jnp.full((E, C + 1), S, jnp.int32).at[e_grid, slot].set(t_grid)
            idx = buf[:, :C]
            valid = idx < S
            x_pad = jnp.concatenate([xf, jnp.zeros((1, d), xf.dtype)], axis=0)
            xin = x_pad[idx]
            h = jax.nn.relu(jnp.einsum('ecd,edh->ech', xin, w1) + b1[:, None, :])
            out = jnp.einsum('ech,ehd->ecd', h, w2) + b2[:, None, :]
            w_pad = jnp.concatenate([w_te, jnp.zeros((1, E), xf.dtype)], axis=0)
            tok_w = w_pad[idx, jnp.arange(E)[:, None]]
            out = out * jnp.where(valid, tok_w, 0.0)[:, :, None]
            final = jnp.zeros((S + 1, d), xf.dtype).at[idx.reshape(-1)].add(out.reshape(-1, d))[:S]
            return final.reshape(Bb, Tt, d)
        key = jax.random.key(seed)
        ks = jax.random.split(key, 7)
        s = 0.02
        return {'x': jax.random.normal(ks[0], (B, T, D_MODEL), jnp.float32), 'gate_w': jax.random.normal(ks[1], (D_MODEL, E), jnp.float32) * s, 'gate_b': jnp.zeros((E,), jnp.float32), 'w1': jax.random.normal(ks[2], (E, D_MODEL, FF), jnp.float32) * s, 'b1': jnp.zeros((E, FF), jnp.float32), 'w2': jax.random.normal(ks[3], (E, FF, D_MODEL), jnp.float32) * s, 'b2': jnp.zeros((E, D_MODEL), jnp.float32)}
    _L0_ffn_in = _L0_ffn_setup()
    _d = {'L0_attn_hidden_states': _L0_attn_in['hidden_states'], 'L0_attn_Wq': _L0_attn_in['Wq'], 'L0_attn_Wk': _L0_attn_in['Wk'], 'L0_attn_Wv': _L0_attn_in['Wv'], 'L0_attn_Wa': _L0_attn_in['Wa'], 'L0_attn_ba': _L0_attn_in['ba'], 'L0_attn_Wb': _L0_attn_in['Wb'], 'L0_attn_bb': _L0_attn_in['bb'], 'L0_attn_conv_q_w': _L0_attn_in['conv_q_w'], 'L0_attn_conv_q_b': _L0_attn_in['conv_q_b'], 'L0_attn_conv_k_w': _L0_attn_in['conv_k_w'], 'L0_attn_conv_k_b': _L0_attn_in['conv_k_b'], 'L0_attn_conv_v_w': _L0_attn_in['conv_v_w'], 'L0_attn_conv_v_b': _L0_attn_in['conv_v_b'], 'L0_attn_Wg': _L0_attn_in['Wg'], 'L0_attn_bg': _L0_attn_in['bg'], 'L0_attn_Wo': _L0_attn_in['Wo'], 'L0_ffn_gate_w': _L0_ffn_in['gate_w'], 'L0_ffn_gate_b': _L0_ffn_in['gate_b'], 'L0_ffn_w1': _L0_ffn_in['w1'], 'L0_ffn_b1': _L0_ffn_in['b1'], 'L0_ffn_w2': _L0_ffn_in['w2'], 'L0_ffn_b2': _L0_ffn_in['b2']}
    _x0 = _d['L0_attn_hidden_states']
    _d['L0_attn_hidden_states'] = jax.random.normal(jax.random.fold_in(jax.random.key(seed), 1), (4, 1024, 128), dtype=_x0.dtype)
    del _x0
    return _d

def reference(L0_attn_hidden_states, L0_attn_Wq, L0_attn_Wk, L0_attn_Wv, L0_attn_Wa, L0_attn_ba, L0_attn_Wb, L0_attn_bb, L0_attn_conv_q_w, L0_attn_conv_q_b, L0_attn_conv_k_w, L0_attn_conv_k_b, L0_attn_conv_v_w, L0_attn_conv_v_b, L0_attn_Wg, L0_attn_bg, L0_attn_Wo, L0_ffn_gate_w, L0_ffn_gate_b, L0_ffn_w1, L0_ffn_b1, L0_ffn_w2, L0_ffn_b2):

    def _L0_attn_ref(hidden_states, Wq, Wk, Wv, Wa, ba, Wb, bb, conv_q_w, conv_q_b, conv_k_w, conv_k_b, conv_v_w, conv_v_b, Wg, bg, Wo):
        import jax, jax.numpy as jnp
        import numpy as np
        D = 128
        H = 16
        DH = 64
        K = 4
        C = H * DH

        def _causal_conv(x, w, b):
            y = jax.lax.conv_general_dilated(x, w, window_strides=(1,), padding=[(K - 1, 0)], feature_group_count=C, dimension_numbers=('NCH', 'OIH', 'NCH'))
            return y + b[None, :, None]
        B, T, _ = hidden_states.shape
        q = jnp.einsum('btd,cd->bct', hidden_states, Wq)
        k = jnp.einsum('btd,cd->bct', hidden_states, Wk)
        v = jnp.einsum('btd,cd->bct', hidden_states, Wv)
        q = jax.nn.silu(_causal_conv(q, conv_q_w, conv_q_b))
        k = jax.nn.silu(_causal_conv(k, conv_k_w, conv_k_b))
        v = jax.nn.silu(_causal_conv(v, conv_v_w, conv_v_b))
        q = q.transpose(0, 2, 1).reshape(B, T, H, DH)
        k = k.transpose(0, 2, 1).reshape(B, T, H, DH)
        v = v.transpose(0, 2, 1).reshape(B, T, H, DH)
        k = k / jnp.maximum(jnp.linalg.norm(k, axis=-1, keepdims=True), 1e-12)
        alpha = jax.nn.sigmoid(jnp.einsum('btd,hd->bth', hidden_states, Wa) + ba)
        beta = jax.nn.sigmoid(jnp.einsum('btd,hd->bth', hidden_states, Wb) + bb)

        def step(S, xs):
            kt, vt, qt, at, bt = xs
            v_old = jnp.einsum('bhij,bhj->bhi', S, kt)
            upd = vt - at[..., None] * v_old
            dS = upd[..., :, None] * kt[..., None, :]
            S = jnp.clip(at[..., None, None] * S + bt[..., None, None] * dS, -5.0, 5.0)
            ot = jnp.einsum('bhij,bhj->bhi', S, qt)
            return (S, ot)
        S0 = jnp.zeros((B, H, DH, DH), hidden_states.dtype)
        xs = (k.transpose(1, 0, 2, 3), v.transpose(1, 0, 2, 3), q.transpose(1, 0, 2, 3), alpha.transpose(1, 0, 2), beta.transpose(1, 0, 2))
        _, ys = jax.lax.scan(step, S0, xs)
        y = ys.transpose(1, 0, 2, 3).reshape(B, T, C)
        g = jax.nn.silu(jnp.einsum('btd,cd->btc', hidden_states, Wg) + bg)
        y = y * g
        out = jnp.einsum('btc,dc->btd', y, Wo)
        return out

    def _L0_ffn_ref(x, gate_w, gate_b, w1, b1, w2, b2):
        import jax, jax.numpy as jnp
        import numpy as np
        D_MODEL = 128
        FF = 512
        E = 8
        TOP_K = 2
        CAP_FACTOR = 1.25
        B, T = (4, 256)

        def _moe_forward(x, gate_w, gate_b, w1, b1, w2, b2):
            Bb, Tt, d = x.shape
            S = Bb * Tt
            C = int(CAP_FACTOR * S / E)
            xf = x.reshape(S, d)
            logits = xf @ gate_w + gate_b
            probs = jax.nn.softmax(logits, axis=1)
            topk_p, topk_i = jax.lax.top_k(probs, TOP_K)
            topk_pn = topk_p / jnp.sum(topk_p, axis=1, keepdims=True)
            rows = jnp.arange(S)
            w_te = jnp.zeros((S, E), xf.dtype).at[rows[:, None], topk_i].set(topk_pn)
            mask = jnp.zeros((S, E), bool).at[rows[:, None], topk_i].set(True)
            rank = jnp.cumsum(mask.astype(jnp.int32), axis=0)
            slot = jnp.where(mask & (rank <= C), rank - 1, C)
            e_grid = jnp.broadcast_to(jnp.arange(E), (S, E))
            t_grid = jnp.broadcast_to(rows[:, None], (S, E))
            buf = jnp.full((E, C + 1), S, jnp.int32).at[e_grid, slot].set(t_grid)
            idx = buf[:, :C]
            valid = idx < S
            x_pad = jnp.concatenate([xf, jnp.zeros((1, d), xf.dtype)], axis=0)
            xin = x_pad[idx]
            h = jax.nn.relu(jnp.einsum('ecd,edh->ech', xin, w1) + b1[:, None, :])
            out = jnp.einsum('ech,ehd->ecd', h, w2) + b2[:, None, :]
            w_pad = jnp.concatenate([w_te, jnp.zeros((1, E), xf.dtype)], axis=0)
            tok_w = w_pad[idx, jnp.arange(E)[:, None]]
            out = out * jnp.where(valid, tok_w, 0.0)[:, :, None]
            final = jnp.zeros((S + 1, d), xf.dtype).at[idx.reshape(-1)].add(out.reshape(-1, d))[:S]
            return final.reshape(Bb, Tt, d)
        return _moe_forward(x, gate_w, gate_b, w1, b1, w2, b2)
    x = L0_attn_hidden_states
    xn = _layernorm(x, axis=-1)
    x = x + _L0_attn_ref(xn, L0_attn_Wq, L0_attn_Wk, L0_attn_Wv, L0_attn_Wa, L0_attn_ba, L0_attn_Wb, L0_attn_bb, L0_attn_conv_q_w, L0_attn_conv_q_b, L0_attn_conv_k_w, L0_attn_conv_k_b, L0_attn_conv_v_w, L0_attn_conv_v_b, L0_attn_Wg, L0_attn_bg, L0_attn_Wo) + _L0_ffn_ref(xn, L0_ffn_gate_w, L0_ffn_gate_b, L0_ffn_w1, L0_ffn_b1, L0_ffn_w2, L0_ffn_b2)
    return x

_drawn_inputs = setup_inputs


def setup_inputs(seed=0):
    import zlib

    import numpy as np

    out = dict(_drawn_inputs(seed))
    spreads = {'L0_attn_ba': (0.0, 0.8),
     'L0_attn_bb': (0.0, 0.8),
     'L0_attn_conv_q_b': (0.0, 0.8),
     'L0_attn_conv_k_b': (0.0, 0.8),
     'L0_attn_conv_v_b': (0.0, 0.8),
     'L0_attn_bg': (0.0, 0.8),
     'L0_ffn_gate_b': (0.0, 0.1),
     'L0_ffn_b1': (0.0, 0.49),
     'L0_ffn_b2': (0.0, 0.34)}
    factors = {'L0_attn_Wq': 8.0,
     'L0_attn_Wk': 8.0,
     'L0_attn_Wv': 8.0,
     'L0_attn_Wa': 8.0,
     'L0_attn_Wb': 8.0,
     'L0_attn_conv_q_w': 8.0,
     'L0_attn_conv_k_w': 8.0,
     'L0_attn_conv_v_w': 8.0,
     'L0_attn_Wg': 8.0,
     'L0_attn_Wo': 8.0,
     'L0_ffn_w1': 3.428}
    for name, (base, spread) in spreads.items():
        noise = np.random.default_rng([zlib.crc32(name.encode()), seed]).standard_normal(out[name].shape)
        drawn = base * np.exp(spread * noise) if base else spread * noise
        out[name] = jnp.asarray(drawn.astype(out[name].dtype))
    for name, factor in factors.items():
        out[name] = (out[name] * factor).astype(out[name].dtype)
    return out
```

```python
from contextlib import ExitStack

import concourse.bass as bass
from concourse import mybir

F32 = mybir.dt.float32
ALU = mybir.AluOpType
ACT = mybir.ActivationFunctionType
AX = mybir.AxisListType

B, T, D = 4, 1024, 128
H, DH = 16, 64
C = H * DH
TAPS = 4
E, FF = 8, 512
P = 128
S = B * T
NT = S // P
GT = 512 // P
NG = NT // GT
HP = C // P
KF = FF // P
CAPACITY = int(1.25 * S / E)
LN_EPS = 1e-5
NORM_EPS = 1e-12
CLIP = 5.0


class Tally:

    def __init__(self, sem, base=0, step=1):
        self.sem, self.base, self.step, self.n = sem, base, step, 0

    def on(self, ins):
        ins.then_inc(self.sem, self.step)
        self.n += self.step
        return self.n

    def wait(self, eng, n=None):
        eng.wait_ge(self.sem, self.base + (self.n if n is None else n))


def norm_and_route(nc, ctx, ps, x, xT, res, wte, ident, dram):
    def sb(name, shape):
        return c2.enter_context(nc.sbuf_tensor(name, shape, F32))

    with ExitStack() as c2:
        sem = lambda name: ctx.enter_context(nc.semaphore(name))
        xn = sb("xn", [P, NT, D])
        stats = sb("stats", [P, NT, 6])
        meanvar = sb("meanvar", [P, NT, 2])
        rstd = sb("rstd", [P, NT])
        gate_w = sb("gate_w", [P, E])
        gate_b = sb("gate_b", [1, E])
        ones = sb("ones", [P, P])
        upto = sb("upto", [P, P])
        w_ab = sb("w_ab", [P, 2 * H])
        b_ab = sb("b_ab", [2 * H, 1])
        ab = sb("ab", [2 * H, S])
        prob = sb("prob", [P, NT, E])
        top = sb("top", [P, NT])
        beats = sb("beats", [P, E, NT, E])
        place = sb("place", [P, E, NT])
        chosen = sb("chosen", [P, NT, E])
        count = sb("count", [P, NT, E])
        total = sb("total", [P, NT, E])
        before = sb("before", [P, NT, E])
        x_in, small_in, ab_out = sem("x_in"), sem("small_in"), sem("ab_out")
        consts, var_ready, std_ready = sem("consts"), sem("var_ready"), sem("std_ready")
        xn_ready, xT_ps, xT_ready = sem("xn_ready"), sem("xT_ps"), sem("xT_ready")
        logit_ps, logit_max, prob_ready = sem("logit_ps"), sem("logit_max"), sem("prob_ready")
        ab_ps, ab_ready = sem("ab_ps"), sem("ab_ready")
        chosen_ready, count_ps, dve_chain = sem("chosen_ready"), sem("count_ps"), sem("dve_chain")
        pool_chain = sem("pool_chain")
        block = c2.enter_context(nc.Block())
        x_tiles = x.rearrange("b (n p) d -> p (b n) d", p=P)

        @block.sync
        def _(sp):
            for g in range(NG):
                sp.dma_start(res[:, g * GT:(g + 1) * GT, :], x_tiles[:, g * GT:(g + 1) * GT, :]).then_inc(x_in, 16)
                sp.wait_ge(x_in, 16 * (g + 1))
            sp.dma_start(gate_w[:], dram["gate_w"]).then_inc(small_in, 16)
            sp.dma_start(gate_b[:], dram["gate_b"].rearrange("(a e) -> a e", a=1)).then_inc(small_in, 16)
            sp.dma_start(w_ab[:, 0:H], dram["WaT"]).then_inc(small_in, 16)
            sp.dma_start(w_ab[:, H:2 * H], dram["WbT"]).then_inc(small_in, 16)
            sp.dma_start(b_ab[0:H, :], dram["ba"].rearrange("(h a) -> h a", a=1)).then_inc(small_in, 16)
            sp.dma_start(b_ab[H:2 * H, :], dram["bb"].rearrange("(h a) -> h a", a=1)).then_inc(small_in, 16)
            sp.wait_ge(ab_ready, NG)
            sp.dma_start(dram["ab"], ab[:]).then_inc(ab_out, 16)
            sp.wait_ge(ab_out, 16)

        @block.gpsimd
        def _(pool):
            chain = Tally(pool_chain)
            chain.on(nc.gpsimd.memset(ident[:], 0.0))
            chain.on(nc.gpsimd.memset(upto[:], 1.0))
            nc.gpsimd.memset(ones[:], 1.0).then_inc(consts, 1)
            chain.wait(pool)
            nc.gpsimd.affine_select(out=ident[:], in_=ident[:], compare_op=ALU.not_equal, fill=1.0, base=0,
                                    pattern=[[-1, P]], channel_multiplier=1).then_inc(consts, 1)
            nc.gpsimd.affine_select(out=upto[:], in_=upto[:], compare_op=ALU.is_ge, fill=0.0, base=0,
                                    pattern=[[1, P]], channel_multiplier=-1).then_inc(consts, 1)
            nc.gpsimd.memset(beats[:], 0.0).then_inc(consts, 1)

        @block.vector
        def _(dve):
            chain = Tally(dve_chain)
            for n in range(NT):
                if n % GT == 0:
                    dve.wait_ge(x_in, 16 * (n // GT + 1))
                chain.on(nc.vector.bn_stats(stats[:, n, :], res[:, n, :]))
            chain.wait(dve)
            for n in range(NT):
                chain.on(nc.vector.bn_aggr(meanvar[:, n, :], stats[:, n, :]))
            chain.wait(dve)
            nc.vector.tensor_scalar(rstd[:], meanvar[:, :, 1], LN_EPS, None, ALU.add).then_inc(var_ready, 1)
            dve.wait_ge(std_ready, 1)
            chain.on(nc.vector.reciprocal(rstd[:], rstd[:]))
            chain.wait(dve)
            for n in range(NT):
                nc.vector.tensor_scalar(xn[:, n, :], res[:, n, :], meanvar[:, n, 0:1], rstd[:, n:n + 1],
                                        ALU.subtract, ALU.mult).then_inc(xn_ready, 1)
            dve.wait_ge(logit_ps, 1)
            logits = ps[6][:, 0:NT * E].rearrange("p (n e) -> p n e", e=E)
            chain.on(nc.vector.tensor_reduce(top[:], logits, AX.X, ALU.max))
            chain.wait(dve)
            nc.vector.tensor_tensor(prob[:], logits, top[:].unsqueeze(2).broadcast_to([P, NT, E]),
                                    ALU.subtract).then_inc(logit_max, 1)
            dve.wait_ge(prob_ready, 1)
            chain.on(nc.vector.tensor_reduce(top[:], prob[:], AX.X, ALU.add))
            chain.wait(dve)
            chain.on(nc.vector.reciprocal(top[:], top[:]))
            chain.wait(dve)
            chain.on(nc.vector.tensor_tensor(prob[:], prob[:], top[:].unsqueeze(2).broadcast_to([P, NT, E]), ALU.mult))
            chain.wait(dve)
            dve.wait_ge(consts, 4)
            for e in range(E):
                if e:
                    chain.on(nc.vector.tensor_tensor(beats[:, e, :, 0:e], prob[:, :, 0:e],
                                                     prob[:, :, e:e + 1].broadcast_to([P, NT, e]), ALU.is_ge))
                if e < E - 1:
                    chain.on(nc.vector.tensor_tensor(beats[:, e, :, e + 1:E], prob[:, :, e + 1:E],
                                                     prob[:, :, e:e + 1].broadcast_to([P, NT, E - 1 - e]), ALU.is_gt))
            chain.wait(dve)
            chain.on(nc.vector.tensor_reduce(place[:], beats[:], AX.X, ALU.add))
            chain.wait(dve)
            nc.vector.tensor_scalar(chosen[:], place[:].rearrange("p e n -> p n e"), 1.5, None,
                                    ALU.is_lt).then_inc(chosen_ready, 1)
            dve.wait_ge(chosen_ready, 1)
            chain.on(nc.vector.tensor_tensor(prob[:], prob[:], chosen[:], ALU.mult))
            chain.wait(dve)
            chain.on(nc.vector.tensor_reduce(top[:], prob[:], AX.X, ALU.add))
            chain.wait(dve)
            chain.on(nc.vector.reciprocal(top[:], top[:]))
            chain.wait(dve)
            chain.on(nc.vector.tensor_tensor(prob[:], prob[:], top[:].unsqueeze(2).broadcast_to([P, NT, E]), ALU.mult))
            dve.wait_ge(count_ps, 1)
            chain.on(nc.vector.tensor_copy(count[:], ps[7][:, 0:NT * E].rearrange("p (n e) -> p n e", e=E)))
            chain.on(nc.vector.tensor_copy(total[:], ps[7][:, NT * E:2 * NT * E].rearrange("p (n e) -> p n e", e=E)))
            chain.on(nc.vector.memset(before[:, 0, :], 0.0))
            chain.wait(dve)
            for n in range(1, NT):
                chain.on(nc.vector.tensor_tensor(before[:, n, :], before[:, n - 1, :], total[:, n - 1, :], ALU.add))
                chain.wait(dve)
            chain.on(nc.vector.tensor_tensor(count[:], count[:], before[:], ALU.add))
            chain.wait(dve)
            chain.on(nc.vector.tensor_scalar(count[:], count[:], float(CAPACITY) + 0.5, None, ALU.is_lt))
            chain.wait(dve)
            chain.on(nc.vector.tensor_tensor(wte[:], prob[:], count[:], ALU.mult))
            chain.wait(dve)

        @block.scalar
        def _(act):
            act.wait_ge(var_ready, 1)
            nc.scalar.activation(rstd[:], rstd[:], ACT.Sqrt).then_inc(std_ready, 1)
            for g in range(NG):
                act.wait_ge(xT_ps, g + 1)
                nc.scalar.activation(xT[:, g * 512:(g + 1) * 512], ps[g % 4][:], ACT.Copy).then_inc(xT_ready, 1)
            act.wait_ge(logit_max, 1)
            nc.scalar.activation(prob[:], prob[:], ACT.Exp).then_inc(prob_ready, 1)
            for g in range(NG):
                act.wait_ge(ab_ps, g + 1)
                nc.scalar.activation(ab[:, g * 512:(g + 1) * 512], ps[4 + g % 2][0:2 * H, :], ACT.Sigmoid,
                                     bias=b_ab[:]).then_inc(ab_ready, 1)

        @block.tensor
        def _(pe):
            pe.wait_ge(consts, 3)
            for g in range(NG):
                pe.wait_ge(xn_ready, (g + 1) * GT)
                if g >= 4:
                    pe.wait_ge(xT_ready, g - 3)
                for j in range(GT):
                    last = nc.tensor.transpose(ps[g % 4][:, j * P:(j + 1) * P], xn[:, g * GT + j, :], ident[:])
                last.then_inc(xT_ps, 1)
            pe.wait_ge(small_in, 16 * 6)
            for n in range(NT):
                if n % GT == 0:
                    pe.wait_ge(xT_ready, n // GT + 1)
                out = ps[6][:, n * E:(n + 1) * E]
                nc.tensor.matmul(out, xT[:, n * P:(n + 1) * P], gate_w[:], start=True, stop=False)
                last = nc.tensor.matmul(out, ones[0:1, :], gate_b[:], start=False, stop=True)
            last.then_inc(logit_ps, 1)
            for g in range(NG):
                if g >= 2:
                    pe.wait_ge(ab_ready, g - 1)
                nc.tensor.matmul(ps[4 + g % 2][0:2 * H, :], w_ab[:], xT[:, g * 512:(g + 1) * 512],
                                 start=True, stop=True).then_inc(ab_ps, 1)
            pe.wait_ge(chosen_ready, 1)
            flat = chosen[:].rearrange("p n e -> p (n e)")
            nc.tensor.matmul(ps[7][:, 0:NT * E], upto[:], flat, start=True, stop=True)
            nc.tensor.matmul(ps[7][:, NT * E:2 * NT * E], ones[:], flat, start=True, stop=True).then_inc(count_ps, 1)


def experts(nc, ctx, ps, xT, res, wte, ident, dram):
    with ExitStack() as c2:
        def sb(name, shape):
            return c2.enter_context(nc.sbuf_tensor(name, shape, F32))
        sem = lambda name: ctx.enter_context(nc.semaphore(name))
        w1 = sb("w1", [P, E, FF])
        w2 = sb("w2", [P, E, KF, D])
        b1_rows = sb("b1_rows", [E * KF, P])
        b1 = sb("b1", [P, E * KF])
        b2 = sb("b2", [E, D])
        wteT = sb("wteT", [E, S])
        hidden = sb("hidden", [P, 2, KF, 512])
        w_in, b_in = sem("w_in"), sem("b_in")
        setup_ps, setup_ready = sem("setup_ps"), sem("setup_ready")
        bias_ps, bias_added = sem("bias_ps"), sem("bias_added")
        h_ps, h_ready, out_ps, out_added = sem("h_ps"), sem("h_ready"), sem("out_ps"), sem("out_added")
        block = c2.enter_context(nc.Block())

        @block.sync
        def _(sp):
            sp.dma_start(b1_rows[:], dram["b1"].rearrange("e (k f) -> (e k) f", f=P)).then_inc(b_in, 16)
            sp.dma_start(b2[:], dram["b2"]).then_inc(b_in, 16)
            sp.dma_start(w1[:], dram["w1"].rearrange("e d f -> d e f")).then_inc(w_in, 16)
            sp.dma_start(w2[:], dram["w2"].rearrange("e (k f) d -> f e k d", f=P)).then_inc(w_in, 16)

        @block.tensor
        def _(pe):
            pe.wait_ge(b_in, 32)
            nc.tensor.transpose(ps[0][:, 0:E * KF], b1_rows[:], ident[0:E * KF, 0:E * KF]).then_inc(setup_ps, 1)
            for g in range(NG):
                if g >= 2:
                    pe.wait_ge(setup_ready, g)
                for j in range(GT):
                    last = nc.tensor.transpose(ps[1 + g % 2][0:E, j * P:(j + 1) * P], wte[:, g * GT + j, :], ident[:])
                last.then_inc(setup_ps, 1)
            for g in range(NG):
                pe.wait_ge(setup_ready, g + 2)
                if g >= 2:
                    pe.wait_ge(bias_added, g - 1)
                for j in range(GT):
                    n = g * GT + j
                    last = nc.tensor.matmul(ps[6 + g % 2][:, j * P:(j + 1) * P], wteT[:, n * P:(n + 1) * P], b2[:],
                                            start=True, stop=True)
                last.then_inc(bias_ps, 1)
            pe.wait_ge(w_in, 32)
            pe.wait_ge(bias_added, NG)
            pe.wait_ge(setup_ready, NG + 1)
            for i in range(NG * E + 1):
                if i < NG * E:
                    g, e = divmod(i, E)
                    for k in range(KF):
                        u = i * KF + k
                        if u >= 4:
                            pe.wait_ge(h_ready, u - 3)
                        nc.tensor.matmul(ps[u % 4][:], w1[:, e, k * P:(k + 1) * P], xT[:, g * 512:(g + 1) * 512],
                                         start=True, stop=True).then_inc(h_ps, 1)
                if i >= 1:
                    o = i - 1
                    e = o % E
                    pe.wait_ge(h_ready, (o + 1) * KF)
                    if o >= 2:
                        pe.wait_ge(out_added, o - 1)
                    for j in range(GT):
                        for k in range(KF):
                            last = nc.tensor.matmul(ps[4 + o % 2][:, j * P:(j + 1) * P],
                                                    hidden[:, o % 2, k, j * P:(j + 1) * P], w2[:, e, k, :],
                                                    start=(k == 0), stop=(k == KF - 1))
                    last.then_inc(out_ps, 1)

        @block.scalar
        def _(act):
            act.wait_ge(setup_ps, 1)
            nc.scalar.activation(b1[:], ps[0][:, 0:E * KF], ACT.Copy).then_inc(setup_ready, 1)
            for g in range(NG):
                act.wait_ge(setup_ps, g + 2)
                nc.scalar.activation(wteT[:, g * 512:(g + 1) * 512], ps[1 + g % 2][0:E, :], ACT.Copy).then_inc(setup_ready, 1)
            act.wait_ge(setup_ready, NG + 1)
            for i in range(NG * E):
                e = i % E
                if i >= 2:
                    act.wait_ge(out_ps, i - 1)
                for k in range(KF):
                    u = i * KF + k
                    act.wait_ge(h_ps, u + 1)
                    nc.scalar.activation(hidden[:, i % 2, k, :], ps[u % 4][:], ACT.Relu,
                                         bias=b1[:, e * KF + k:e * KF + k + 1]).then_inc(h_ready, 1)

        @block.vector
        def _(dve):
            for g in range(NG):
                dve.wait_ge(bias_ps, g + 1)
                rows = res[:, g * GT:(g + 1) * GT, :]
                nc.vector.tensor_tensor(rows, rows, ps[6 + g % 2][:].rearrange("p (j d) -> p j d", d=D),
                                        ALU.add).then_inc(bias_added, 1)
            dve.wait_ge(bias_added, NG)
            for i in range(NG * E):
                g, e = divmod(i, E)
                dve.wait_ge(out_ps, i + 1)
                if e:
                    dve.wait_ge(out_added, i)
                for j in range(GT):
                    n = g * GT + j
                    last = nc.vector.scalar_tensor_tensor(out=res[:, n, :], in0=ps[4 + i % 2][:, j * P:(j + 1) * P],
                                                          scalar=wte[:, n, e:e + 1], in1=res[:, n, :],
                                                          op0=ALU.mult, op1=ALU.add)
                last.then_inc(out_added, 1)


def project(nc, ctx, ps, xT, dram):
    STEPS = 3 * B
    NBUF = 3
    with ExitStack() as c2:
        def sb(name, shape):
            return c2.enter_context(nc.sbuf_tensor(name, shape, F32))
        sem = lambda name: ctx.enter_context(nc.semaphore(name))
        w = sb("w_qkv", [P, 3, P])
        taps = sb("taps", [P, HP, 3, TAPS])
        bias = sb("conv_bias", [P, HP, 3])
        tap_now = sb("tap_now", [P, 3, TAPS])
        bias_now = sb("bias_now", [P, 3])
        pre = sb("pre", [P, 2, TAPS - 1 + T])
        conv = sb("conv", [P, 2, T])
        act_out = sb("act_out", [P, NBUF, T])
        w_in, taps_in = [sem(f"w_in{a}") for a in range(3)], sem("taps_in")
        proj_ps, pre_ready, conv_ready = sem("proj_ps"), sem("pre_ready"), sem("conv_ready")
        conv_chain, qkv_ready = sem("conv_chain"), sem("qkv_ready")
        stored = [sem(f"stored{i}") for i in range(NBUF)]
        now_ready, pads = sem("now_ready"), sem("pads")
        block = c2.enter_context(nc.Block())
        names = ("q", "k", "v")

        @block.sync
        def _(sp):
            with nc.allow_non_contiguous_dma("taps and biases are small"):
                for a, name in enumerate(names):
                    sp.dma_start(taps[:, :, a, :], dram["conv_%s_w" % name].rearrange("(h p) o k -> p h (o k)", p=P)).then_inc(taps_in, 16)
                    sp.dma_start(bias[:, :, a], dram["conv_%s_b" % name].rearrange("(h p) -> p h", p=P)).then_inc(taps_in, 16)
            sp.sem_inc(proj_ps, 2 * STEPS)
            with nc.sync.Fori(0, HP) as hp:
                for a, name in enumerate(names):
                    sp.wait_ge(proj_ps, hp * (2 * STEPS) + 2 * B * (a + 1))
                    sp.dma_start(w[:, a, :], dram["W%sT" % name][:, bass.ts(hp, P)]).then_inc(w_in[a], 16)
                for i in range(STEPS):
                    a, b = divmod(i, B)
                    sp.wait_ge(qkv_ready, hp * STEPS + i + 1 + 2)
                    sp.dma_start(dram["qkv"][a, bass.ts(hp, P), b * T:(b + 1) * T], act_out[:, i % NBUF, :]).then_inc(stored[i % NBUF], 16)
            for i in range(NBUF):
                sp.wait_ge(stored[i], HP * (STEPS // NBUF) * 16 + 16)

        @block.tensor
        def _(pe):
            pe.sem_inc(pre_ready, 4)
            with nc.tensor.Fori(0, HP) as hp:
                for i in range(STEPS):
                    a, b = divmod(i, B)
                    if b == 0:
                        pe.wait_ge(w_in[a], hp * 16 + 16)
                    pe.wait_ge(pre_ready, hp * (2 * STEPS) + 2 * i + 2)
                    for half in range(2):
                        ins = nc.tensor.matmul(ps[4 * (i % 2) + half][:], w[:, a, :],
                                               xT[:, b * T + half * 512:b * T + (half + 1) * 512], start=True, stop=True)
                        ins.then_inc(proj_ps, 1)

        @block.scalar
        def _(act):
            act.wait_ge(pads, 1)
            act.sem_inc(conv_ready, 2)
            for i in range(NBUF):
                act.sem_inc(stored[i], 16)
            with nc.scalar.Fori(0, HP) as hp:
                for i in range(STEPS + 1):
                    if i < STEPS:
                        act.wait_ge(conv_ready, hp * STEPS + i + 1)
                        for half in range(2):
                            act.wait_ge(proj_ps, hp * (2 * STEPS) + 2 * i + half + 1 + 2 * STEPS)
                            nc.scalar.activation(pre[:, i % 2, TAPS - 1 + half * 512:TAPS - 1 + (half + 1) * 512],
                                                 ps[4 * (i % 2) + half][:], ACT.Copy).then_inc(pre_ready, 1)
                    if i:
                        o = i - 1
                        act.wait_ge(conv_ready, hp * STEPS + o + 1 + 2)
                        act.wait_ge(stored[o % NBUF], (hp * (STEPS // NBUF) + o // NBUF) * 16 + 16)
                        nc.scalar.activation(act_out[:, o % NBUF, :], conv[:, o % 2, :], ACT.Silu,
                                             bias=bias_now[:, o // B:o // B + 1]).then_inc(qkv_ready, 1)

        @block.vector
        def _(dve):
            nc.vector.memset(pre[:, :, 0:TAPS - 1], 0.0).then_inc(pads, 1)
            dve.wait_ge(taps_in, 6 * 16)
            dve.sem_inc(qkv_ready, 2)
            with nc.vector.Fori(0, HP) as hp:
                dve.wait_ge(qkv_ready, hp * STEPS + 2)
                nc.vector.tensor_copy(tap_now[:], taps[:, bass.ds(hp, 1), :, :].rearrange("p o a k -> p (o a) k")).then_inc(now_ready, 1)
                nc.vector.tensor_copy(bias_now[:], bias[:, bass.ds(hp, 1), :].rearrange("p o a -> p (o a)")).then_inc(now_ready, 1)
                dve.wait_ge(now_ready, hp * 2 + 2)
                for i in range(STEPS):
                    a = i // B
                    dve.wait_ge(pre_ready, hp * (2 * STEPS) + 2 * i + 2 + 4)
                    dve.wait_ge(qkv_ready, hp * STEPS + i + 1)
                    nc.vector.tensor_scalar(conv[:, i % 2, :], pre[:, i % 2, 0:T], tap_now[:, a, 0:1], None,
                                            ALU.mult).then_inc(conv_chain, 1)
                    for j in range(1, TAPS):
                        dve.wait_ge(conv_chain, hp * (STEPS * (TAPS - 1)) + i * (TAPS - 1) + j)
                        nc.vector.scalar_tensor_tensor(out=conv[:, i % 2, :], in0=pre[:, i % 2, j:j + T],
                                                       scalar=tap_now[:, a, j:j + 1], in1=conv[:, i % 2, :],
                                                       op0=ALU.mult, op1=ALU.add)\
                            .then_inc(conv_ready if j == TAPS - 1 else conv_chain, 1)


def replay(nc, ctx, dram, tag=""):
    HALF = DH // 2
    TB = 32
    NB = T // TB
    G = B * H
    with ExitStack() as c2:
        def sb(name, shape):
            return c2.enter_context(nc.sbuf_tensor(name + tag, shape, F32))
        sem = lambda name: ctx.enter_context(nc.semaphore(name + tag))
        ab = sb("ab_all", [P, 2, T])
        qk = sb("qk", [P, 2, 2, DH, TB])
        v = sb("vrow", [P, 2, HALF, TB])
        y = sb("yrow", [P, 2, HALF, TB])
        a_now, na_now, b_now = sb("a_now", [P, TB]), sb("na_now", [P, TB]), sb("b_now", [P, TB])
        sq = sb("sq", [P, DH, TB])
        norm = sb("norm", [P, TB])
        state = sb("state", [P, HALF, DH])
        prod = sb("prod", [P, HALF, DH])
        qprod = sb("qprod", [P, 2, HALF, DH])
        old = sb("old", [P, HALF])
        upd = sb("upd", [P, HALF])
        ab_in, norm_sq, norm_root = sem("ab_all_in"), sem("norm_sq"), sem("norm_root")
        blk_in = [sem(f"blk_in{i}") for i in range(2)]
        y_out = [sem(f"y_out{i}") for i in range(2)]
        y_ready, chain_s, state_ready, qprod_ready = sem("y_ready"), sem("step_chain"), sem("state_ready"), sem("qprod_ready")
        LOADS = 2 * B * 3
        block = c2.enter_context(nc.Block())
        rows = lambda half, b: slice(half * G + b * H, half * G + (b + 1) * H)

        @block.sync
        def _(sp):
            for half in range(2):
                for b in range(B):
                    for i in range(2):
                        sp.dma_start(ab[rows(half, b), i, :], dram["ab"][i * H:(i + 1) * H, b * T:(b + 1) * T]).then_inc(ab_in, 16)
            sp.sem_inc(y_ready, 2)
            with nc.sync.Fori(0, NB // 2) as it:
                for par in range(2):
                    sp.wait_ge(y_ready, it * 2 + par + 1)
                    for half in range(2):
                        for b in range(B):
                            tok = bass.ds(it * (2 * TB) + (b * T + par * TB), TB)
                            for i in range(2):
                                sp.dma_start(qk[rows(half, b), par, i, :, :],
                                             dram["qkv"][i, :, tok].rearrange("(h j) t -> h j t", h=H)).then_inc(blk_in[par], 16)
                            sp.dma_start(v[rows(half, b), par, :, :],
                                         dram["qkv"][2, :, tok].rearrange("(h g i) t -> g h i t", h=H, g=2)[half]).then_inc(blk_in[par], 16)

        @block.gpsimd
        def _(pool):
            with nc.gpsimd.Fori(0, NB // 2) as it:
                for t in range(2 * TB):
                    par, tt = divmod(t, TB)
                    pool.wait_ge(state_ready, it * (2 * TB) + t + 1)
                    nc.gpsimd.tensor_tensor(qprod[:, t % 2, :, :], state[:],
                                            qk[:, par, 0, :, tt:tt + 1].rearrange("p j o -> p o j").broadcast_to([P, HALF, DH]),
                                            ALU.mult).then_inc(qprod_ready, 1)

        @block.scalar
        def _(act):
            with nc.scalar.Fori(0, NB // 2) as it:
                for par in range(2):
                    act.wait_ge(norm_sq, it * 2 + par + 1)
                    nc.scalar.activation(norm[:], norm[:], ACT.Sqrt).then_inc(norm_root, 1)
                    act.wait_ge(y_ready, it * 2 + par + 1 + 2)
                    for half in range(2):
                        for b in range(B):
                            tok = bass.ds(it * (2 * TB) + (b * T + par * TB), TB)
                            act.dma_start(dram["yT"][:, tok].rearrange("(h g i) t -> g h i t", h=H, g=2)[half],
                                          y[rows(half, b), par, :, :]).then_inc(y_out[par], 16)
            for par in range(2):
                act.wait_ge(y_out[par], NB // 2 * 2 * B * 16 + 16)

        @block.vector
        def _(dve):
            PER = 2 * (7 + 5 * TB)
            dve.wait_ge(ab_in, 4 * B * 16)
            nc.vector.memset(state[:], 0.0).then_inc(chain_s, 1)
            dve.sem_inc(qprod_ready, 1)
            for par in range(2):
                dve.sem_inc(y_out[par], 16)
            with nc.vector.Fori(0, NB // 2) as it:
                chain = Tally(chain_s, base=it * PER + 1)
                for par in range(2):
                    dve.wait_ge(blk_in[par], it * (LOADS * 16) + LOADS * 16)
                    cols = bass.ds(it * (2 * TB) + par * TB, TB)
                    chain.on(nc.vector.tensor_copy(a_now[:], ab[:, 0, cols]))
                    chain.on(nc.vector.tensor_copy(b_now[:], ab[:, 1, cols]))
                    chain.wait(dve)
                    chain.on(nc.vector.tensor_scalar(na_now[:], a_now[:], -1.0, None, ALU.mult))
                    kk = qk[:, par, 1, :, :]
                    chain.on(nc.vector.tensor_tensor(sq[:], kk, kk, ALU.mult))
                    chain.wait(dve)
                    nc.vector.tensor_reduce(norm[:], sq[:].rearrange("p j t -> p t j"), AX.X, ALU.add).then_inc(norm_sq, 1)
                    dve.wait_ge(norm_root, it * 2 + par + 1)
                    chain.on(nc.vector.tensor_scalar(norm[:], norm[:], NORM_EPS, None, ALU.max))
                    chain.wait(dve)
                    chain.on(nc.vector.reciprocal(norm[:], norm[:]))
                    chain.wait(dve)
                    chain.on(nc.vector.tensor_tensor(kk, kk, norm[:].unsqueeze(1).broadcast_to([P, DH, TB]), ALU.mult))
                    chain.wait(dve)
                    dve.wait_ge(y_out[par], it * (2 * B * 16) + 16)
                    for tt in range(TB):
                        t = par * TB + tt
                        k_t = qk[:, par, 1, :, tt:tt + 1].rearrange("p j o -> p o j").broadcast_to([P, HALF, DH])
                        chain.on(nc.vector.tensor_tensor(prod[:], state[:], k_t, ALU.mult))
                        chain.wait(dve)
                        chain.on(nc.vector.tensor_reduce(old[:], prod[:], AX.X, ALU.add))
                        chain.wait(dve)
                        chain.on(nc.vector.scalar_tensor_tensor(out=upd[:], in0=old[:], scalar=na_now[:, tt:tt + 1],
                                                                in1=v[:, par, :, tt], op0=ALU.mult, op1=ALU.add))
                        chain.wait(dve)
                        chain.on(nc.vector.scalar_tensor_tensor(out=prod[:], in0=upd[:].unsqueeze(2).broadcast_to([P, HALF, DH]),
                                                                scalar=b_now[:, tt:tt + 1], in1=k_t, op0=ALU.mult, op1=ALU.mult))
                        chain.wait(dve)
                        dve.wait_ge(qprod_ready, it * (2 * TB) + t + 1)
                        chain.on(nc.vector.scalar_tensor_tensor(out=state[:], in0=state[:], scalar=a_now[:, tt:tt + 1],
                                                                in1=prod[:], op0=ALU.mult, op1=ALU.add))
                        chain.wait(dve)
                        nc.vector.tensor_scalar(state[:], state[:], CLIP, -CLIP, ALU.min, ALU.max).then_inc(state_ready, 1)
                        dve.wait_ge(state_ready, it * (2 * TB) + t + 1)
                        if tt >= 1:
                            dve.wait_ge(qprod_ready, it * (2 * TB) + t + 1)
                            nc.vector.tensor_reduce(y[:, par, :, tt - 1], qprod[:, (t - 1) % 2, :, :], AX.X, ALU.add)
                    dve.wait_ge(qprod_ready, it * (2 * TB) + (par + 1) * TB + 1)
                    nc.vector.tensor_reduce(y[:, par, :, TB - 1], qprod[:, (TB - 1) % 2, :, :], AX.X, ALU.add).then_inc(y_ready, 1)
                assert chain.n == PER, (chain.n, PER)


def gate_and_output(nc, ctx, ps, xT, res, dram, out):
    with ExitStack() as c2:
        def sb(name, shape):
            return c2.enter_context(nc.sbuf_tensor(name, shape, F32))
        sem = lambda name: ctx.enter_context(nc.semaphore(name))
        wg = sb("wg", [P, C])
        wo = sb("wo", [P, HP, D])
        bg = sb("bg", [P, HP])
        yt = sb("yt", [P, 2, HP, 512])
        gate = sb("gate", [P, 2, HP, 512])
        w_in, g_ps, g_ready = sem("wgo_in"), sem("g_ps"), sem("g_ready")
        y_in = [sem(f"y_in{i}") for i in range(2)]
        gated, o_ps, o_ready, o_out = sem("gated"), sem("o_ps"), sem("o_ready"), sem("o_out")
        block = c2.enter_context(nc.Block())
        out_tiles = out.rearrange("b (n p) d -> p (b n) d", p=P)

        @block.sync
        def _(sp):
            sp.dma_start(wg[:], dram["WgT"]).then_inc(w_in, 16)
            sp.dma_start(wo[:], dram["WoT"].rearrange("(h p) d -> p h d", p=P)).then_inc(w_in, 16)
            with nc.allow_non_contiguous_dma("bg is small"):
                sp.dma_start(bg[:], dram["bg"].rearrange("(h p) -> p h", p=P)).then_inc(w_in, 16)
            for g in range(NG):
                if g >= 2:
                    sp.wait_ge(gated, (g - 1) * HP)
                sp.dma_start(yt[:, g % 2, :, :], dram["yT"][:, g * 512:(g + 1) * 512].rearrange("(h p) t -> p h t", p=P)).then_inc(y_in[g % 2], 16)

        @block.gpsimd
        def _(pool):
            for g in range(NG):
                pool.wait_ge(o_ready, g + 1)
                pool.dma_start(out_tiles[:, g * GT:(g + 1) * GT, :], res[:, g * GT:(g + 1) * GT, :]).then_inc(o_out, 16)
            pool.wait_ge(o_out, 16 * NG)

        @block.tensor
        def _(pe):
            pe.wait_ge(w_in, 48)
            for g in range(NG + 1):
                if g < NG:
                    for hp in range(HP):
                        u = g * HP + hp
                        if u >= 4:
                            pe.wait_ge(g_ready, u - 3)
                        nc.tensor.matmul(ps[u % 4][:], wg[:, hp * P:(hp + 1) * P], xT[:, g * 512:(g + 1) * 512],
                                         start=True, stop=True).then_inc(g_ps, 1)
                if g >= 1:
                    o = g - 1
                    pe.wait_ge(gated, (o + 1) * HP)
                    if o >= 2:
                        pe.wait_ge(o_ready, o - 1)
                    for j in range(GT):
                        for hp in range(HP):
                            last = nc.tensor.matmul(ps[4 + o % 2][:, j * P:(j + 1) * P], gate[:, o % 2, hp, j * P:(j + 1) * P],
                                                    wo[:, hp, :], start=(hp == 0), stop=(hp == HP - 1))
                    last.then_inc(o_ps, 1)

        @block.scalar
        def _(act):
            act.wait_ge(w_in, 48)
            for g in range(NG):
                if g >= 2:
                    act.wait_ge(o_ps, g - 1)
                for hp in range(HP):
                    u = g * HP + hp
                    act.wait_ge(g_ps, u + 1)
                    nc.scalar.activation(gate[:, g % 2, hp, :], ps[u % 4][:], ACT.Silu, bias=bg[:, hp:hp + 1]).then_inc(g_ready, 1)

        @block.vector
        def _(dve):
            for g in range(NG):
                dve.wait_ge(y_in[g % 2], (g // 2 + 1) * 16)
                for hp in range(HP):
                    dve.wait_ge(g_ready, g * HP + hp + 1)
                    nc.vector.tensor_tensor(gate[:, g % 2, hp, :], gate[:, g % 2, hp, :], yt[:, g % 2, hp, :],
                                            ALU.mult).then_inc(gated, 1)
                dve.wait_ge(o_ps, g + 1)
                rows = res[:, g * GT:(g + 1) * GT, :]
                nc.vector.tensor_tensor(rows, rows, ps[4 + g % 2][:].rearrange("p (j d) -> p j d", d=D),
                                        ALU.add).then_inc(o_ready, 1)


def build(nc, x, dram, out):
    with ExitStack() as ctx:
        ps = [ctx.enter_context(nc.psum_tensor(f"ps{i}", [P, 512], F32)) for i in range(8)]
        xT = ctx.enter_context(nc.sbuf_tensor("xT", [P, S], F32))
        res = ctx.enter_context(nc.sbuf_tensor("res", [P, NT, D], F32))
        wte = ctx.enter_context(nc.sbuf_tensor("wte", [P, NT, E], F32))
        ident = ctx.enter_context(nc.sbuf_tensor("ident", [P, P], F32))
        norm_and_route(nc, ctx, ps, x, xT, res, wte, ident, dram)
        experts(nc, ctx, ps, xT, res, wte, ident, dram)
        project(nc, ctx, ps, xT, dram)
        replay(nc, ctx, dram)
        gate_and_output(nc, ctx, ps, xT, res, dram, out)


def kernel(**inputs):
    import numpy as np
    import concourse.bacc as bacc
    from concourse.bass_utils import run_bass_kernel_spmd

    attn = {k[len("L0_attn_"):]: v for k, v in inputs.items() if k.startswith("L0_attn_")}
    ffn = {k[len("L0_ffn_"):]: v for k, v in inputs.items() if k.startswith("L0_ffn_")}
    laid = {"x": attn["hidden_states"]}
    for name in ("Wq", "Wk", "Wv", "Wa", "Wb", "Wg", "Wo"):
        laid[name + "T"] = np.transpose(attn[name])
    for name in ("ba", "bb", "bg", "conv_q_w", "conv_q_b", "conv_k_w", "conv_k_b", "conv_v_w", "conv_v_b"):
        laid[name] = attn[name]
    laid.update(ffn)

    nc = bacc.Bacc("TRN2", target_bir_lowering=False, num_devices=1)
    arrays, dram = {}, {}
    for name, a in laid.items():
        a = np.ascontiguousarray(a)
        arrays["in_" + name] = a
        dram[name] = nc.dram_tensor("in_" + name, a.shape, mybir.dt.from_np(a.dtype), kind="ExternalInput").ap()
    out = nc.dram_tensor("out_0", (B, T, D), F32, kind="ExternalOutput").ap()
    dram["ab"] = nc.dram_tensor("ab_scratch", (2 * H, S), F32, kind="Internal").ap()
    dram["qkv"] = nc.dram_tensor("qkv_scratch", (3, C, S), F32, kind="Internal").ap()
    dram["yT"] = nc.dram_tensor("y_scratch", (C, S), F32, kind="Internal").ap()
    build(nc, dram["x"], dram, out)
    got = run_bass_kernel_spmd(nc, [arrays], core_ids=[0])
    return got.results[0]["out_0"]
```

```python
from contextlib import ExitStack

import concourse.bass as bass
from concourse import mybir

F32 = mybir.dt.float32
ALU = mybir.AluOpType
ACT = mybir.ActivationFunctionType
AX = mybir.AxisListType

B, T, D = 4, 1024, 128
H, DH = 16, 64
C = H * DH
TAPS = 4
E, FF = 8, 512
P = 128
S = B * T
NT = S // P
GT = 512 // P
NG = NT // GT
HP = C // P
KF = FF // P
CAPACITY = int(1.25 * S / E)
LN_EPS = 1e-5
NORM_EPS = 1e-12
CLIP = 5.0
FALLBACK = True


class Tally:

    def __init__(self, sem, base=0, step=1):
        self.sem, self.base, self.step, self.n = sem, base, step, 0

    def on(self, ins):
        ins.then_inc(self.sem, self.step)
        self.n += self.step
        return self.n

    def wait(self, eng, n=None):
        eng.wait_ge(self.sem, self.base + (self.n if n is None else n))


def norm_and_route(nc, ctx, ps, x, xT, res, wte, ident, gates, dram):
    def sb(name, shape):
        return c2.enter_context(nc.sbuf_tensor(name, shape, F32))

    with ExitStack() as c2:
        sem = lambda name: ctx.enter_context(nc.semaphore(name))
        xn = sb("xn", [P, NT, D])
        stats = sb("stats", [P, NT, 6])
        meanvar = sb("meanvar", [P, NT, 2])
        rstd = sb("rstd", [P, NT])
        gate_w = sb("gate_w", [P, E])
        gate_b = sb("gate_b", [1, E])
        ones = sb("ones", [P, P])
        upto = sb("upto", [P, P])
        w_ab = sb("w_ab", [P, 2 * H])
        b_ab = sb("b_ab", [2 * H, 1])
        b_ab_row = sb("b_ab_row", [1, 2 * H])
        decay_x = sb("decay_x", [P, NT, H])
        softplus = sb("softplus", [P, NT, H])
        ab = sb("ab", [2 * H, S])
        prob = sb("prob", [P, NT, E])
        top = sb("top", [P, NT])
        beats = sb("beats", [P, E, NT, E])
        place = sb("place", [P, E, NT])
        chosen = sb("chosen", [P, NT, E])
        count = sb("count", [P, NT, E])
        total = sb("total", [P, NT, E])
        before = sb("before", [P, NT, E])
        x_in, small_in, ab_out = sem("x_in"), sem("small_in"), sem("ab_out")
        consts, var_ready, std_ready = sem("consts"), sem("var_ready"), sem("std_ready")
        xn_ready, xT_ps, xT_ready = sem("xn_ready"), sem("xT_ps"), sem("xT_ready")
        logit_ps, logit_max, prob_ready = sem("logit_ps"), sem("logit_max"), sem("prob_ready")
        ab_ps, ab_ready = sem("ab_ps"), sem("ab_ready")
        chosen_ready, count_ps, dve_chain = sem("chosen_ready"), sem("count_ps"), sem("dve_chain")
        pool_chain = sem("pool_chain")
        gate_ps, clamped, exp_ready, softplus_ready, logs_ready, cumlog_ps = [
            sem(n) for n in ("gate_ps", "clamped", "exp_ready", "softplus_ready", "logs_ready", "cumlog_ps")]
        log_decay, beta, neg_cumlog = gates
        block = c2.enter_context(nc.Block())
        x_tiles = x.rearrange("b (n p) d -> p (b n) d", p=P)

        @block.sync
        def _(sp):
            for g in range(NG):
                sp.dma_start(res[:, g * GT:(g + 1) * GT, :], x_tiles[:, g * GT:(g + 1) * GT, :]).then_inc(x_in, 16)
                sp.wait_ge(x_in, 16 * (g + 1))
            sp.dma_start(gate_w[:], dram["gate_w"]).then_inc(small_in, 16)
            sp.dma_start(gate_b[:], dram["gate_b"].rearrange("(a e) -> a e", a=1)).then_inc(small_in, 16)
            sp.dma_start(w_ab[:, 0:H], dram["WaT"]).then_inc(small_in, 16)
            sp.dma_start(w_ab[:, H:2 * H], dram["WbT"]).then_inc(small_in, 16)
            sp.dma_start(b_ab[0:H, :], dram["ba"].rearrange("(h a) -> h a", a=1)).then_inc(small_in, 16)
            sp.dma_start(b_ab[H:2 * H, :], dram["bb"].rearrange("(h a) -> h a", a=1)).then_inc(small_in, 16)
            sp.dma_start(b_ab_row[:, 0:H], dram["ba"].rearrange("(a h) -> a h", a=1)).then_inc(small_in, 16)
            sp.dma_start(b_ab_row[:, H:2 * H], dram["bb"].rearrange("(a h) -> a h", a=1)).then_inc(small_in, 16)
            sp.wait_ge(ab_ready, NG)
            sp.dma_start(dram["ab"], ab[:]).then_inc(ab_out, 16)
            sp.wait_ge(ab_out, 16)

        @block.gpsimd
        def _(pool):
            chain = Tally(pool_chain)
            chain.on(nc.gpsimd.memset(ident[:], 0.0))
            chain.on(nc.gpsimd.memset(upto[:], 1.0))
            nc.gpsimd.memset(ones[:], 1.0).then_inc(consts, 1)
            chain.wait(pool)
            nc.gpsimd.affine_select(out=ident[:], in_=ident[:], compare_op=ALU.not_equal, fill=1.0, base=0,
                                    pattern=[[-1, P]], channel_multiplier=1).then_inc(consts, 1)
            nc.gpsimd.affine_select(out=upto[:], in_=upto[:], compare_op=ALU.is_ge, fill=0.0, base=0,
                                    pattern=[[1, P]], channel_multiplier=-1).then_inc(consts, 1)
            nc.gpsimd.memset(beats[:], 0.0).then_inc(consts, 1)

        @block.vector
        def _(dve):
            chain = Tally(dve_chain)
            for n in range(NT):
                if n % GT == 0:
                    dve.wait_ge(x_in, 16 * (n // GT + 1))
                chain.on(nc.vector.bn_stats(stats[:, n, :], res[:, n, :]))
            chain.wait(dve)
            for n in range(NT):
                chain.on(nc.vector.bn_aggr(meanvar[:, n, :], stats[:, n, :]))
            chain.wait(dve)
            nc.vector.tensor_scalar(rstd[:], meanvar[:, :, 1], LN_EPS, None, ALU.add).then_inc(var_ready, 1)
            dve.wait_ge(std_ready, 1)
            chain.on(nc.vector.reciprocal(rstd[:], rstd[:]))
            chain.wait(dve)
            for n in range(NT):
                nc.vector.tensor_scalar(xn[:, n, :], res[:, n, :], meanvar[:, n, 0:1], rstd[:, n:n + 1],
                                        ALU.subtract, ALU.mult).then_inc(xn_ready, 1)
            dve.wait_ge(gate_ps, 1)
            for i in range(2):
                half = slice(i * NT // 2, (i + 1) * NT // 2)
                raw = ps[i][:].rearrange("p (n g) -> p n g", g=2 * H)[:, :, 0:H]
                chain.on(nc.vector.tensor_scalar(softplus[:, half, :], raw, -40.0, None, ALU.max))
                chain.wait(dve)
                nc.vector.tensor_tensor(decay_x[:, half, :], raw, softplus[:, half, :], ALU.subtract).then_inc(clamped, 1)
            dve.wait_ge(softplus_ready, 1)
            dve.wait_ge(clamped, 2)
            nc.vector.tensor_tensor(log_decay[:], decay_x[:], softplus[:], ALU.subtract).then_inc(logs_ready, 1)
            dve.wait_ge(logit_ps, 1)
            logits = ps[6][:, 0:NT * E].rearrange("p (n e) -> p n e", e=E)
            chain.on(nc.vector.tensor_reduce(top[:], logits, AX.X, ALU.max))
            chain.wait(dve)
            nc.vector.tensor_tensor(prob[:], logits, top[:].unsqueeze(2).broadcast_to([P, NT, E]),
                                    ALU.subtract).then_inc(logit_max, 1)
            dve.wait_ge(prob_ready, 1)
            chain.on(nc.vector.tensor_reduce(top[:], prob[:], AX.X, ALU.add))
            chain.wait(dve)
            chain.on(nc.vector.reciprocal(top[:], top[:]))
            chain.wait(dve)
            chain.on(nc.vector.tensor_tensor(prob[:], prob[:], top[:].unsqueeze(2).broadcast_to([P, NT, E]), ALU.mult))
            chain.wait(dve)
            dve.wait_ge(consts, 4)
            for e in range(E):
                if e:
                    chain.on(nc.vector.tensor_tensor(beats[:, e, :, 0:e], prob[:, :, 0:e],
                                                     prob[:, :, e:e + 1].broadcast_to([P, NT, e]), ALU.is_ge))
                if e < E - 1:
                    chain.on(nc.vector.tensor_tensor(beats[:, e, :, e + 1:E], prob[:, :, e + 1:E],
                                                     prob[:, :, e:e + 1].broadcast_to([P, NT, E - 1 - e]), ALU.is_gt))
            chain.wait(dve)
            chain.on(nc.vector.tensor_reduce(place[:], beats[:], AX.X, ALU.add))
            chain.wait(dve)
            nc.vector.tensor_scalar(chosen[:], place[:].rearrange("p e n -> p n e"), 1.5, None,
                                    ALU.is_lt).then_inc(chosen_ready, 1)
            dve.wait_ge(chosen_ready, 1)
            chain.on(nc.vector.tensor_tensor(prob[:], prob[:], chosen[:], ALU.mult))
            chain.wait(dve)
            chain.on(nc.vector.tensor_reduce(top[:], prob[:], AX.X, ALU.add))
            chain.wait(dve)
            chain.on(nc.vector.reciprocal(top[:], top[:]))
            chain.wait(dve)
            chain.on(nc.vector.tensor_tensor(prob[:], prob[:], top[:].unsqueeze(2).broadcast_to([P, NT, E]), ALU.mult))
            dve.wait_ge(count_ps, 1)
            chain.on(nc.vector.tensor_copy(count[:], ps[7][:, 0:NT * E].rearrange("p (n e) -> p n e", e=E)))
            chain.on(nc.vector.tensor_copy(total[:], ps[7][:, NT * E:2 * NT * E].rearrange("p (n e) -> p n e", e=E)))
            chain.on(nc.vector.memset(before[:, 0, :], 0.0))
            chain.wait(dve)
            for n in range(1, NT):
                chain.on(nc.vector.tensor_tensor(before[:, n, :], before[:, n - 1, :], total[:, n - 1, :], ALU.add))
                chain.wait(dve)
            chain.on(nc.vector.tensor_tensor(count[:], count[:], before[:], ALU.add))
            chain.wait(dve)
            chain.on(nc.vector.tensor_scalar(count[:], count[:], float(CAPACITY) + 0.5, None, ALU.is_lt))
            chain.wait(dve)
            chain.on(nc.vector.tensor_tensor(wte[:], prob[:], count[:], ALU.mult))
            chain.wait(dve)

        @block.scalar
        def _(act):
            act.wait_ge(var_ready, 1)
            nc.scalar.activation(rstd[:], rstd[:], ACT.Sqrt).then_inc(std_ready, 1)
            for g in range(NG):
                act.wait_ge(xT_ps, g + 1)
                nc.scalar.activation(xT[:, g * 512:(g + 1) * 512], ps[g % 4][:], ACT.Copy).then_inc(xT_ready, 1)
            act.wait_ge(clamped, 2)
            for i in range(2):
                half = slice(i * NT // 2, (i + 1) * NT // 2)
                nc.scalar.activation(beta[:, half, :], ps[i][:].rearrange("p (n g) -> p n g", g=2 * H)[:, :, H:2 * H],
                                     ACT.Sigmoid)
            act.wait_ge(clamped, 2)
            nc.scalar.activation(softplus[:], softplus[:], ACT.Exp, scale=-1.0).then_inc(exp_ready, 1)
            act.wait_ge(exp_ready, 1)
            nc.scalar.activation(softplus[:], softplus[:], ACT.Ln, bias=1.0).then_inc(softplus_ready, 1)
            act.wait_ge(cumlog_ps, 1)
            nc.scalar.activation(neg_cumlog[:], ps[2][:].rearrange("p (n h) -> p n h", h=H), ACT.Copy, scale=-1.0)
            act.wait_ge(logit_max, 1)
            nc.scalar.activation(prob[:], prob[:], ACT.Exp).then_inc(prob_ready, 1)
            for g in range(NG):
                act.wait_ge(ab_ps, g + 1)
                nc.scalar.activation(ab[:, g * 512:(g + 1) * 512], ps[4 + g % 2][0:2 * H, :], ACT.Sigmoid,
                                     bias=b_ab[:]).then_inc(ab_ready, 1)

        @block.tensor
        def _(pe):
            pe.wait_ge(consts, 3)
            for g in range(NG):
                pe.wait_ge(xn_ready, (g + 1) * GT)
                if g >= 4:
                    pe.wait_ge(xT_ready, g - 3)
                for j in range(GT):
                    last = nc.tensor.transpose(ps[g % 4][:, j * P:(j + 1) * P], xn[:, g * GT + j, :], ident[:])
                last.then_inc(xT_ps, 1)
            pe.wait_ge(small_in, 16 * 8)
            for n in range(NT):
                if n % GT == 0:
                    pe.wait_ge(xT_ready, n // GT + 1)
                out = ps[6][:, n * E:(n + 1) * E]
                nc.tensor.matmul(out, xT[:, n * P:(n + 1) * P], gate_w[:], start=True, stop=False)
                last = nc.tensor.matmul(out, ones[0:1, :], gate_b[:], start=False, stop=True)
            last.then_inc(logit_ps, 1)
            pe.wait_ge(xT_ready, NG)
            for n in range(NT):
                out = ps[2 * n // NT][:, n % (NT // 2) * 2 * H:(n % (NT // 2) + 1) * 2 * H]
                nc.tensor.matmul(out, xT[:, n * P:(n + 1) * P], w_ab[:], start=True, stop=False)
                last = nc.tensor.matmul(out, ones[0:1, :], b_ab_row[:], start=False, stop=True)
            last.then_inc(gate_ps, 1)
            pe.wait_ge(logs_ready, 1)
            nc.tensor.matmul(ps[2][:], upto[:], log_decay[:].rearrange("p n h -> p (n h)"),
                             start=True, stop=True).then_inc(cumlog_ps, 1)
            for g in range(NG):
                if g >= 2:
                    pe.wait_ge(ab_ready, g - 1)
                nc.tensor.matmul(ps[4 + g % 2][0:2 * H, :], w_ab[:], xT[:, g * 512:(g + 1) * 512],
                                 start=True, stop=True).then_inc(ab_ps, 1)
            pe.wait_ge(chosen_ready, 1)
            flat = chosen[:].rearrange("p n e -> p (n e)")
            nc.tensor.matmul(ps[7][:, 0:NT * E], upto[:], flat, start=True, stop=True)
            nc.tensor.matmul(ps[7][:, NT * E:2 * NT * E], ones[:], flat, start=True, stop=True).then_inc(count_ps, 1)


def expert_biases(nc, ctx, ps, res, wte, b1, ident, dram):
    with ExitStack() as c2:
        def sb(name, shape):
            return c2.enter_context(nc.sbuf_tensor(name, shape, F32))
        sem = lambda name: ctx.enter_context(nc.semaphore(name))
        b1_rows = sb("b1_rows", [E * KF, P])
        b2 = sb("b2", [E, D])
        wteT = sb("wteT", [E, S])
        b_in, setup_ps, setup_ready = sem("b_in"), sem("setup_ps"), sem("setup_ready")
        bias_ps, bias_added = sem("bias_ps"), sem("bias_added")
        block = c2.enter_context(nc.Block())

        @block.sync
        def _(sp):
            sp.dma_start(b1_rows[:], dram["b1"].rearrange("e (k f) -> (e k) f", f=P)).then_inc(b_in, 16)
            sp.dma_start(b2[:], dram["b2"]).then_inc(b_in, 16)

        @block.tensor
        def _(pe):
            pe.wait_ge(b_in, 32)
            nc.tensor.transpose(ps[0][:, 0:E * KF], b1_rows[:], ident[0:E * KF, 0:E * KF]).then_inc(setup_ps, 1)
            for g in range(NG):
                if g >= 2:
                    pe.wait_ge(setup_ready, g)
                for j in range(GT):
                    last = nc.tensor.transpose(ps[1 + g % 2][0:E, j * P:(j + 1) * P], wte[:, g * GT + j, :], ident[:])
                last.then_inc(setup_ps, 1)
            for g in range(NG):
                pe.wait_ge(setup_ready, g + 2)
                if g >= 2:
                    pe.wait_ge(bias_added, g - 1)
                for j in range(GT):
                    n = g * GT + j
                    last = nc.tensor.matmul(ps[6 + g % 2][:, j * P:(j + 1) * P], wteT[:, n * P:(n + 1) * P], b2[:],
                                            start=True, stop=True)
                last.then_inc(bias_ps, 1)

        @block.scalar
        def _(act):
            act.wait_ge(setup_ps, 1)
            nc.scalar.activation(b1[:], ps[0][:, 0:E * KF], ACT.Copy).then_inc(setup_ready, 1)
            for g in range(NG):
                act.wait_ge(setup_ps, g + 2)
                nc.scalar.activation(wteT[:, g * 512:(g + 1) * 512], ps[1 + g % 2][0:E, :], ACT.Copy).then_inc(setup_ready, 1)

        @block.vector
        def _(dve):
            for g in range(NG):
                dve.wait_ge(bias_ps, g + 1)
                rows = res[:, g * GT:(g + 1) * GT, :]
                nc.vector.tensor_tensor(rows, rows, ps[6 + g % 2][:].rearrange("p (j d) -> p j d", d=D),
                                        ALU.add).then_inc(bias_added, 1)


def project(nc, ctx, ps, xT, dram):
    STEPS = 3 * B
    NBUF = 3
    with ExitStack() as c2:
        def sb(name, shape):
            return c2.enter_context(nc.sbuf_tensor(name, shape, F32))
        sem = lambda name: ctx.enter_context(nc.semaphore(name))
        w = sb("w_qkv", [P, 3, P])
        taps = sb("taps", [P, HP, 3, TAPS])
        bias = sb("conv_bias", [P, HP, 3])
        tap_now = sb("tap_now", [P, 3, TAPS])
        bias_now = sb("bias_now", [P, 3])
        pre = sb("pre", [P, 2, TAPS - 1 + T])
        conv = sb("conv", [P, 2, T])
        act_out = sb("act_out", [P, NBUF, T])
        w_in, taps_in = [sem(f"w_in{a}") for a in range(3)], sem("taps_in")
        proj_ps, pre_ready, conv_ready = sem("proj_ps"), sem("pre_ready"), sem("conv_ready")
        conv_chain, qkv_ready = sem("conv_chain"), sem("qkv_ready")
        stored = [sem(f"stored{i}") for i in range(NBUF)]
        taps_now, bias_ready, first_tap, pads, apart = sem("taps_now"), sem("bias_ready"), sem("first_tap"), sem("pads"), sem("apart")
        block = c2.enter_context(nc.Block())
        names = ("q", "k", "v")

        @block.sync
        def _(sp):
            with nc.allow_non_contiguous_dma("taps and biases are small"):
                for a, name in enumerate(names):
                    sp.dma_start(taps[:, :, a, :], dram["conv_%s_w" % name].rearrange("(h p) o k -> p h (o k)", p=P)).then_inc(taps_in, 16)
                    sp.dma_start(bias[:, :, a], dram["conv_%s_b" % name].rearrange("(h p) -> p h", p=P)).then_inc(taps_in, 16)
            with nc.sync.Fori(0, HP) as hp:
                for i in range(STEPS):
                    a, b = divmod(i, B)
                    sp.wait_ge(qkv_ready, hp * STEPS + i + 1 + 2)
                    sp.dma_start(dram["qkv"][a, bass.ts(hp, P), b * T:(b + 1) * T], act_out[:, i % NBUF, :]).then_inc(stored[i % NBUF], 16)
            for i in range(NBUF):
                sp.wait_ge(stored[i], HP * (STEPS // NBUF) * 16 + 16)

        @block.gpsimd
        def _(pool):
            pool.sem_inc(proj_ps, 2 * STEPS)
            with nc.gpsimd.Fori(0, HP) as hp:
                for a, name in enumerate(names):
                    pool.wait_ge(proj_ps, hp * (2 * STEPS) + 2 * B * (a + 1))
                    pool.sem_inc(apart, 1)
                    pool.dma_start(w[:, a, :], dram["W%sT" % name][:, bass.ts(hp, P)]).then_inc(w_in[a], 16)

        @block.tensor
        def _(pe):
            pe.sem_inc(pre_ready, 4)
            with nc.tensor.Fori(0, HP) as hp:
                for i in range(STEPS):
                    a, b = divmod(i, B)
                    if b == 0:
                        pe.wait_ge(w_in[a], hp * 16 + 16)
                    pe.wait_ge(pre_ready, hp * (2 * STEPS) + 2 * i + 2)
                    for half in range(2):
                        ins = nc.tensor.matmul(ps[4 * (i % 2) + half][:], w[:, a, :],
                                               xT[:, b * T + half * 512:b * T + (half + 1) * 512], start=True, stop=True)
                        ins.then_inc(proj_ps, 1)

        @block.scalar
        def _(act):
            act.wait_ge(pads, 1)
            act.sem_inc(conv_ready, 2)
            for i in range(NBUF):
                act.sem_inc(stored[i], 16)
            with nc.scalar.Fori(0, HP) as hp:
                for i in range(STEPS + 1):
                    if i < STEPS:
                        act.wait_ge(conv_ready, hp * STEPS + i + 1)
                        for half in range(2):
                            act.wait_ge(proj_ps, hp * (2 * STEPS) + 2 * i + half + 1 + 2 * STEPS)
                            nc.scalar.activation(pre[:, i % 2, TAPS - 1 + half * 512:TAPS - 1 + (half + 1) * 512],
                                                 ps[4 * (i % 2) + half][:], ACT.Copy).then_inc(pre_ready, 1)
                        act.wait_ge(pre_ready, hp * (2 * STEPS) + 2 * i + 2 + 4)
                        act.wait_ge(qkv_ready, hp * STEPS + i + 1)
                        act.wait_ge(taps_now, hp + 1)
                        nc.scalar.activation(conv[:, i % 2, :], pre[:, i % 2, 0:T], ACT.Copy,
                                             scale=tap_now[:, i // B, 0:1]).then_inc(first_tap, 1)
                    if i:
                        o = i - 1
                        act.wait_ge(bias_ready, hp + 1)
                        act.wait_ge(conv_ready, hp * STEPS + o + 1 + 2)
                        act.wait_ge(stored[o % NBUF], (hp * (STEPS // NBUF) + o // NBUF) * 16 + 16)
                        nc.scalar.activation(act_out[:, o % NBUF, :], conv[:, o % 2, :], ACT.Silu,
                                             bias=bias_now[:, o // B:o // B + 1]).then_inc(qkv_ready, 1)

        @block.vector
        def _(dve):
            nc.vector.memset(pre[:, :, 0:TAPS - 1], 0.0).then_inc(pads, 1)
            dve.wait_ge(taps_in, 6 * 16)
            dve.sem_inc(qkv_ready, 2)
            with nc.vector.Fori(0, HP) as hp:
                dve.wait_ge(conv_ready, hp * STEPS + 2)
                nc.vector.tensor_copy(tap_now[:], taps[:, bass.ds(hp, 1), :, :].rearrange("p o a k -> p (o a) k")).then_inc(taps_now, 1)
                for i in range(STEPS):
                    a = i // B
                    dve.wait_ge(first_tap, hp * STEPS + i + 1)
                    for j in range(1, TAPS):
                        if i == 0 and j == TAPS - 1:
                            dve.wait_ge(qkv_ready, hp * STEPS + 2)
                            nc.vector.tensor_copy(bias_now[:], bias[:, bass.ds(hp, 1), :].rearrange("p o a -> p (o a)")).then_inc(bias_ready, 1)
                        if j > 1:
                            dve.wait_ge(conv_chain, hp * (STEPS * (TAPS - 2)) + i * (TAPS - 2) + j - 1)
                        nc.vector.scalar_tensor_tensor(out=conv[:, i % 2, :], in0=pre[:, i % 2, j:j + T],
                                                       scalar=tap_now[:, a, j:j + 1], in1=conv[:, i % 2, :],
                                                       op0=ALU.mult, op1=ALU.add)\
                            .then_inc(conv_ready if j == TAPS - 1 else conv_chain, 1)


def chunked(nc, ctx, PS, ps, xT, res, wte, b1, ident, gates, unsafe, dram):
    CH = T // P
    M4 = 4
    CM = CH * M4
    W = 32
    R = P // W
    BF16 = mybir.dt.bfloat16
    UNITS = HP * B // 2
    assert HP == E
    GU = NG // 2
    NORM_LIMIT = 0.5 * (CLIP * CLIP - 0.1)
    LOG_LIMIT = 1500.0
    PER = dict(qkv_in=48, kv_ps=CH, kv_tok=CH, k_sq=CH, ss_ready=CH, root_ready=1, vec_chain=8, vec_ready=1, mv_ready=CH,
               cum_ps=CH, g_ready=CH, mask_ps=CH, gam_ready=CH, kk_ps=CH, m_ready=CH, kgqg_ready=CH,
               diag_out=2 * 16 * R, diag_in=16, inv_chain=2 * (W - 1) + 1, inv_ready=1, inv_out=32, ring_in0=16 * R * CH // 2,
               ring_in1=16 * R * CH // 2, m32_ready=CH, kk1_ps=CH, p_ready=CH, kg1_ready=CH, w32_ps=CH,
               w32_ready=CH, x32_ps=CH, x2_ready=CH, t32_ps=CH, t2_ready=CH, w64_ps=CH, w64_ready=CH, x64_ps=CH, x64_ready=CH,
               gam2_ready=CH, z0_ps=CH, r_ready=CH, z_ps=CH, u_ready=CH, uc_ready=CH, s_ps=CH, sg_ready=CH, s_ready=CH,
               y_ps=CH, y_ready=CH, y_out=16 * 2, w1_ps=CH, t1_ready=CH, a1_ready=CH, norm_chain=4 * CH, st1_ready=CH, s1_ready=CH, inc_ready=CH,
               st2_ready=CH, nsq_ps=CH, nmax_ready=CH, end_check=1,
               w_in=32, moe_vecs=1, h_ps=GU * KF, h_ready=GU * KF, out_ps=GU, out_added=GU)
    with ExitStack() as c2:
        def sb(name, shape, dt=F32):
            return c2.enter_context(nc.sbuf_tensor(name, shape, dt))
        sems = {name: ctx.enter_context(nc.semaphore("c_" + name)) for name in PER}
        sem = lambda name: ctx.enter_context(nc.semaphore(name))
        q, k, v = [sb(n + "_in", [P, 2, T]) for n in "qkv"]
        tok = sb("kv_tok", [P, CH, 2, 2, P])
        sq = sb("k_sq", [P, 2, 2, P])
        la, bt, ng = [sb(n, [P, CM]) for n in ("la_unit", "bt_unit", "ng_unit")]
        ss = sb("ss", [P, CM, 2])
        root, inv_n2, c_m, neg_c, half_ss1, half_ss = [
            sb(n, [P, CM]) for n in ("root", "inv_n2", "c_m", "neg_c", "half_ss1", "half_ss")]
        gb = sb("gb", [P, 2, 2, P])
        gb2 = sb("gb2", [P, CH, 2, P])
        kg, qg = sb("kg", [P, CH, 2, P]), sb("qg", [P, CH, 2, P])
        g_end = sb("g_end", [P, CH, 2])
        gam = sb("gam", [P, CM, P])
        neg_m = sb("neg_m", [P, CM, P])
        upto2 = sb("upto2", [P, P])
        mask_bf, ident_bf = sb("mask_bf", [P, M4 * P], BF16), sb("ident_bf", [P, P], BF16)
        diag = sb("diag_in_sb", [P, W, W])
        xb = sb("x_base", [P, 2, W, W])
        prod = sb("x_prod", [P, W, W])
        ring = sb("ring", [P, 2, 2, M4, P])
        m32 = sb("m32", [P, 2, M4, P])
        w32 = sb("w32", [P, M4, P])
        late = sb("late", [P, 8, M4 * P])
        hidden = late[:].rearrange("p (a k) t -> p a k t", a=2)
        pT, kg1, gam2, x2 = [late[:, 2 * i:2 * i + 2, :].rearrange("p a (m t) -> p a m t", m=M4) for i in range(4)]
        w1, w2 = sb("w1", [P, FF]), sb("w2", [P, KF, D])
        b1_now, wte_now = sb("b1_now", [P, KF]), sb("wte_now", [P, GU * GT])
        t2 = sb("t2", [64, M4, 64])
        w64 = sb("w64", [P, M4, 64])
        st = sb("st", [P, 2, 2, P])
        st_g = sb("st_g", [P, 2, P])
        st1 = sb("st1", [P, 2, P])
        st2 = sb("st2", [P, 2, 2 * P])
        r = sb("r", [P, M4, DH])
        u, uc = sb("u", [P, M4, DH]), sb("uc", [P, M4, DH])
        t1, a1 = sb("t1", [P, M4, DH]), sb("a1", [P, M4, DH])
        most = sb("most", [P, CH])
        bad = sb("bad", [P, UNITS * 2 + 1])
        bad_sum = sb("bad_sum", [P, 1])
        ones = sb("ones2", [P, P])
        free = prod[:].rearrange("p a b -> p (a b)")
        scr = free[:, 0:512]
        inc = free[:, 0:512].rearrange("p (m a i) -> p m a i", m=M4, a=2)
        s1, s2 = [free[:, o:o + M4 * DH].rearrange("p (m i) -> p m i", m=M4) for o in (512, 768)]
        setup, setup2, setup3, fin, fin_ps = sem("c_setup"), sem("c_setup2"), sem("c_setup3"), sem("c_fin"), sem("c_fin_ps")
        apart = sem("c_apart")
        log_decay, beta, neg_cumlog = gates
        block = c2.enter_context(nc.Block())
        by_chunk = lambda t: t[:].rearrange("p b (c s) -> p c b s", c=CH)
        kc, qc, vc = by_chunk(k), by_chunk(q), by_chunk(v)
        heads = [slice(0, DH), slice(DH, P)]
        firsts = [slice(0, 32), slice(DH, DH + 32)]
        seconds = [slice(32, DH), slice(DH + 32, P)]
        of = lambda c: slice(c * M4, (c + 1) * M4)
        each = [(b, h, 2 * b + h) for b in range(2) for h in range(2)]
        kk_ps = ((ps[2], ps[5]), (ps[4], ps[6]))
        kv_ps = (ps[0], ps[7])
        cum_ps = (ps[1], ps[3], ps[0])
        pair = lambda kind: PS[:, 3:5, kind * 256:(kind + 1) * 256].rearrange("p h (b t) -> p b h t", b=2)
        by_bh = lambda t: t.rearrange("p (b h) t -> p b h t", h=2)
        m4 = lambda bank: ps[bank][:].rearrange("p (m t) -> p m t", m=M4)

        class At:

            def __init__(self, eng, n):
                self.eng, self.n = eng, n

            def wait(self, name, count):
                self.eng.wait_ge(sems[name], self.n * PER[name] + (PER[name] + count))
                if self.eng is nc.sync:
                    self.apart()

            def apart(self):
                self.eng.sem_inc(apart, 1)

            def inc(self, ins, name, by=1):
                ins.then_inc(sems[name], by)

        def units(eng):
            return eng.Fori(0, HP)

        @block.sync
        def _(sp):
            for name in PER:
                sp.sem_inc(sems[name], PER[name])
            with units(nc.sync) as hp:
                with nc.sync.Fori(0, 2) as bp:
                    e = At(sp, hp * 2 + bp)
                    rows, cols = bass.ts(hp, P), bass.ts(bp, 2 * T)
                    e.wait("kk1_ps", 0)
                    e.wait("kgqg_ready", 0)
                    for i, t in enumerate((q, k, v)):
                        e.inc(sp.dma_start(t[:].rearrange("p b t -> p (b t)"), dram["qkv"][i, rows, cols]), "qkv_in", 16)
                    e.wait("out_ps", 0)
                    e.inc(sp.dma_start(w1[:], dram["w1"][bass.ds(hp, 1), :, :].rearrange("o d f -> d (o f)")), "w_in", 16)
                    e.inc(sp.dma_start(w2[:], dram["w2"][bass.ds(hp, 1), :, :].rearrange("o (k f) d -> f (o k) d", f=P)), "w_in", 16)
                    for c0, c1 in ((0, CH - 2), (CH - 2, CH)):
                        e.wait("m_ready", c1)
                        ms = slice(c0 * M4, c1 * M4)
                        for i in range(R):
                            d = slice(i * W, (i + 1) * W)
                            e.inc(sp.dma_start(dram["diag"][i, ms].rearrange("m (s t) -> s m t", s=W), neg_m[d, ms, d]), "diag_out", 16)
                    e.wait("diag_out", 2 * 16 * R)
                    e.inc(sp.dma_start(diag[:].rearrange("p s t -> p (s t)"), dram["diag"].rearrange("r m x -> (r m) x")), "diag_in", 16)
                    e.wait("inv_ready", 1)
                    for i in range(2):
                        e.inc(sp.dma_start(dram["inverse"].rearrange("r c a m x -> a (r c) m x")[i],
                                           xb[:, i, :, :].rearrange("p s t -> p (s t)")), "inv_out", 16)
                    e.wait("inv_out", 32)
                    for c in range(CH):
                        e.wait("x2_ready", c - 1)
                        e.wait("t2_ready", c - 1)
                        for i in range(R):
                            d = slice(i * W, (i + 1) * W)
                            e.inc(sp.dma_start(ring[d, c % 2, :, :, d].rearrange("s a m t -> s (a m) t"),
                                               dram["inverse"][i, c].rearrange("a m (s t) -> s (a m) t", s=W)),
                                  "ring_in%d" % (c % 2), 16)
            sp.wait_ge(sems["y_out"], (UNITS + 1) * 32)

        @block.tensor
        def _(pe):
            pe.wait_ge(setup, 9)
            pe.wait_ge(setup3, 2)
            mm = nc.tensor.matmul

            def front(e):
                e.wait("qkv_in", 48)
                for name in ("y_ready", "nmax_ready", "x64_ready", "t1_ready", "kg1_ready", "x2_ready"):
                    e.wait(name, 0)
                for c in range(CH):
                    e.wait("kv_tok", c - 1)
                    e.wait("k_sq", c - 1)
                    for i, t in enumerate((kc, vc)):
                        for b in range(2):
                            last = nc.tensor.transpose(kv_ps[c % 2][:, (2 * i + b) * P:(2 * i + b + 1) * P], t[:, c, b, :], ident[:])
                    e.inc(last, "kv_ps")
                e.wait("vec_ready", 1)
                for c in range(CH + 1):
                    if c < CH:
                        e.wait("gam_ready", c - 2)
                        for m in range(M4):
                            last = mm(cum_ps[c % 3][:, m * P:(m + 1) * P], la[:, c * M4 + m:c * M4 + m + 1].broadcast_to([P, P]), upto2[:],
                                      start=(m == 0), stop=(m == M4 - 1), skip_group_check=True)
                        e.inc(last, "cum_ps")
                    if c >= 1:
                        e.wait("g_ready", c)
                        e.inc(mm(cum_ps[(c - 1) % 3], ident_bf[:], mask_bf[:], start=False, stop=True, skip_group_check=True), "mask_ps")
                        o = c - 1
                        e.wait("m_ready", o - 1)
                        for b, h, m in each:
                            last = mm(kk_ps[o % 2][h][:, b * P:(b + 1) * P], kc[heads[h], o, b, :], kc[heads[h], o, b, :], start=True, stop=True)
                        e.inc(last, "kk_ps")

            def moe(e, bp):
                e.wait("m_ready", CH)
                e.wait("gam_ready", CH)
                e.wait("w_in", 32)
                e.wait("inv_chain", 36)
                for g in range(GU + 1):
                    if g < GU:
                        for k in range(KF):
                            u = g * KF + k
                            if u >= 4:
                                e.wait("h_ready", u - 3)
                            e.inc(mm(ps[u % 4], w1[:, k * P:(k + 1) * P], xT[:, bass.ds(bp * (GU * 512) + g * 512, 512)],
                                     start=True, stop=True), "h_ps")
                    if g >= 1:
                        o = g - 1
                        e.wait("h_ready", (o + 1) * KF)
                        for j in range(GT):
                            for k in range(KF):
                                last = mm(ps[4 + o][:, j * P:(j + 1) * P], hidden[:, o % 2, k, j * P:(j + 1) * P], w2[:, k, :],
                                          start=(k == 0), stop=(k == KF - 1))
                        e.inc(last, "out_ps")

            def ahead_a(e, c):
                e.wait("kg1_ready", c)
                if c == 0:
                    e.wait("out_added", GU)
                for b, h, m in each:
                    mm(ps[3 + h][:, b * P:(b + 1) * P], kc[heads[h], c, b, :], qc[heads[h], c, b, :], start=True, stop=True)
                for b, h, m in each:
                    last = mm(ps[3 + h][:, 256 + b * P:256 + (b + 1) * P], kc[firsts[h], c, b, :], kc[firsts[h], c, b, :],
                              start=True, stop=True)
                e.inc(last, "kk1_ps")
                e.wait("m32_ready", c + 1)
                e.wait("ring_in%d" % (c % 2), 16 * R * (c // 2 + 1))
                e.wait("w32_ready", c)
                for m in range(M4):
                    last = mm(ps[0][:, m * P:(m + 1) * P], m32[:, c % 2, m, :], ring[:, c % 2, 1, m, :], start=True, stop=True)
                e.inc(last, "w32_ps")

            def ahead_b(e, c):
                e.wait("w32_ready", c + 1)
                e.wait("x2_ready", c)
                for m in range(M4):
                    last = mm(ps[1][:, m * P:(m + 1) * P], w32[:, m, :], ring[:, c % 2, 0, m, :], start=True, stop=True)
                e.inc(last, "x32_ps")
                e.wait("t2_ready", c)
                e.wait("x64_ready", c)
                e.apart()
                for m in range(M4):
                    last = mm(ps[2][0:64, m * 64:(m + 1) * 64], ring[0:64, c % 2, 0, m, 0:64], w32[0:64, m, 0:64], start=True, stop=True)
                e.inc(last, "t32_ps")

            def ahead_c(e, c):
                e.wait("t2_ready", c + 1)
                e.wait("w64_ready", c)
                e.apart()
                for m in range(M4):
                    last = mm(ps[2][64:128, 256 + m * 64:256 + (m + 1) * 64], neg_m[0:64, c * M4 + m, 64:128], t2[:, m, :],
                              start=True, stop=True)
                e.inc(last, "w64_ps")

            def ahead_d(e, c):
                e.wait("w64_ready", c + 1)
                e.wait("x2_ready", c + 1)
                e.wait("x64_ready", c)
                e.apart()
                for m in range(M4):
                    last = mm(ps[2][0:64, 256 + m * 64:256 + (m + 1) * 64], w64[64:128, m, :], x2[64:128, c % 2, m, 64:128],
                              start=True, stop=True)
                e.inc(last, "x64_ps")

            def chain_z0(e, c):
                e.wait("s_ready", c)
                e.wait("t1_ready", c)
                for b in range(2):
                    last = mm(ps[5][:, b * P:(b + 1) * P], kg[:, c, b, :], st[:, c % 2, b, :], start=True, stop=True)
                e.inc(last, "z0_ps")

            def chain_z(e, c):
                e.wait("r_ready", c + 1)
                e.wait("x64_ready", c + 1)
                for m in range(M4):
                    last = mm(ps[5][:, m * DH:(m + 1) * DH], x2[:, c % 2, m, :], r[:, m, :], start=True, stop=True)
                e.inc(last, "z_ps")

            def chain_s(e, c):
                e.wait("uc_ready", c + 1)
                e.wait("y_ready", c)
                for b, h, m in each:
                    last = mm(ps[6][heads[h], 256 + b * DH:256 + (b + 1) * DH], tok[:, c, 0, b, heads[h]], uc[:, m, :],
                              start=True, stop=True)
                e.inc(last, "s_ps")
                e.wait("nmax_ready", c)
                e.wait("kg1_ready", c + 1)
                e.wait("st1_ready", c + 1)
                for b in range(2):
                    mm(ps[7][:, b * P:(b + 1) * P], kg[:, c, b, :], st1[:, b, :], start=True, stop=False, skip_group_check=True)
                    for h in range(2):
                        m = 2 * b + h
                        last = mm(ps[7][:, m * DH:(m + 1) * DH], kg1[:, c % 2, m, :], u[:, m, :], start=False, stop=True,
                                  skip_group_check=True)
                e.inc(last, "w1_ps")

            def chain_y(e, c):
                e.wait("s_ready", c + 1)
                e.wait("p_ready", c + 1)
                for b in range(2):
                    mm(ps[6][:, b * P:(b + 1) * P], st[:, c % 2, b, :], qg[:, c, b, :], start=True, stop=False, skip_group_check=True)
                    for h in range(2):
                        m = 2 * b + h
                        last = mm(ps[6][heads[h], b * P:(b + 1) * P], u[:, m, :], pT[:, c % 2, m, :], start=False, stop=True,
                                  skip_group_check=True)
                e.inc(last, "y_ps")

            def chain_n(e, c):
                e.wait("inc_ready", c + 1)
                e.wait("st2_ready", c + 1)
                e.wait("gam2_ready", c + 1)
                e.wait("nmax_ready", c)
                for b in range(2):
                    mm(ps[7][:, b * 256:(b + 1) * 256], gb2[:, c, b, :], st2[:, b, :], start=True, stop=False, skip_group_check=True)
                    for h in range(2):
                        m = 2 * b + h
                        last = mm(ps[7][:, m * P:(m + 1) * P], gam2[:, c % 2, m, :], inc[:, m, :, :].rearrange("p a i -> p (a i)"),
                                  start=False, stop=True, skip_group_check=True)
                e.inc(last, "nsq_ps")

            with units(nc.tensor) as hp:
                with nc.tensor.Fori(0, 2) as bp:
                    e = At(pe, hp * 2 + bp)
                    front(e)
                    moe(e, bp)
                    ahead_a(e, 0)
                    ahead_b(e, 0)
                    ahead_c(e, 0)
                    ahead_d(e, 0)
                    for c in range(CH):
                        chain_z0(e, c)
                        if c:
                            chain_n(e, c - 1)
                        if c + 1 < CH:
                            ahead_a(e, c + 1)
                        chain_z(e, c)
                        if c + 1 < CH:
                            ahead_b(e, c + 1)
                        chain_s(e, c)
                        if c + 1 < CH:
                            ahead_c(e, c + 1)
                        chain_y(e, c)
                        if c + 1 < CH:
                            ahead_d(e, c + 1)
                    chain_n(e, CH - 1)
            pe.wait_ge(fin, 1)
            mm(ps[0][:, 0:1], ones[:], bad_sum[:], start=True, stop=True).then_inc(fin_ps, 1)

        @block.scalar
        def _(act):
            fn = nc.scalar.activation
            act.wait_ge(setup, 9)
            with units(nc.scalar) as hp:
                with nc.scalar.Fori(0, 2) as bp:
                    e = At(act, hp * 2 + bp)
                    for c in range(CH):
                        e.wait("kv_ps", c + 1)
                        if c == 0:
                            e.wait("t1_ready", 0)
                            e.wait("s_ps", 0)
                        e.inc(fn(tok[:, c, :, :, :].rearrange("p a b j -> p (a b j)"), kv_ps[c % 2], ACT.Copy), "kv_tok")
                        e.wait("ss_ready", c - 1)
                        e.inc(fn(sq[:, c % 2, :, :].rearrange("p b j -> p (b j)"), kv_ps[c % 2][:, 0:256], ACT.Square), "k_sq")
                    e.wait("vec_chain", 1 + 3)
                    e.inc(fn(root[:], root[:], ACT.Sqrt), "root_ready")
                    e.wait("vec_ready", 1)
                    for c in range(CH + 1):
                        if c < CH:
                            e.wait("cum_ps", c + 1)
                            e.wait("kgqg_ready", c - 1)
                            if c == 0:
                                e.wait("nsq_ps", 0)
                            for h in range(2):
                                src = cum_ps[c % 3].rearrange("p (b h t) -> p b h t", b=2, h=2)[heads[h], :, h, :]
                                fn(gb[heads[h], c % 2, :, :], src, ACT.Exp)
                                last = fn(gb2[heads[h], c, :, :], src, ACT.Exp, scale=2.0)
                            e.inc(last, "g_ready")
                        if c == 0:
                            e.wait("gam2_ready", 0)
                            e.wait("uc_ready", 0)
                            e.wait("kg1_ready", 0)
                            continue
                        e.wait("mask_ps", c)
                        for m in range(M4):
                            cm = (c - 1) * M4 + m
                            last = fn(gam[:, cm, :], cum_ps[(c - 1) % 3][:, m * P:(m + 1) * P], ACT.Exp, bias=ng[:, cm:cm + 1])
                        e.inc(last, "gam_ready")

                    e.wait("moe_vecs", 1)
                    for u in range(GU * KF):
                        g, k = divmod(u, KF)
                        if g >= 2:
                            e.wait("out_ps", g - 1)
                        e.wait("h_ps", u + 1)
                        if u == 0:
                            e.wait("z_ps", 0)
                            e.wait("nsq_ps", 0)
                        e.inc(fn(hidden[:, g % 2, k, :], ps[u % 4], ACT.Relu, bias=b1_now[:, k:k + 1]), "h_ready")
                    e.wait("out_ps", GU)

                    def blocks32(c):
                        e.wait("m_ready", c + 1)
                        e.wait("w32_ps", c - 1)
                        for i in (0, 64):
                            last = fn(m32[i:i + 32, c % 2, :, i + 32:i + 64], neg_m[i:i + 32, of(c), i + 32:i + 64], ACT.Copy)
                        e.inc(last, "m32_ready")

                    def ahead(c):
                        e.wait("w32_ps", c + 1)
                        e.wait("x32_ps", c)
                        e.wait("t32_ps", c)
                        e.inc(fn(w32[:].rearrange("p m t -> p (m t)"), ps[0][:], ACT.Copy), "w32_ready")
                        e.wait("nsq_ps", c - 1)
                        e.inc(fn(gam2[:, c % 2, :, :], gam[:, of(c), :], ACT.Square), "gam2_ready")

                    def ahead2(c):
                        e.wait("w64_ps", c + 1)
                        e.wait("x64_ps", c)
                        e.inc(fn(w64[64:128, :, :], ps[2][64:128, 256:512].rearrange("p (m t) -> p m t", m=M4), ACT.Copy), "w64_ready")

                    def ahead3(c):
                        e.wait("x64_ps", c + 1)
                        e.wait("x2_ready", c + 1)
                        e.inc(fn(x2[0:64, c % 2, :, 64:128], ps[2][0:64, 256:512].rearrange("p (m t) -> p m t", m=M4), ACT.Copy), "x64_ready")

                    blocks32(0)
                    blocks32(1)
                    ahead(0)
                    ahead2(0)
                    ahead3(0)
                    for c in range(CH):
                        if c + 1 < CH:
                            ahead(c + 1)
                        e.wait("s_ready", c)
                        e.wait("w1_ps", c)
                        for h in range(2):
                            last = fn(st1[firsts[h], :, h * DH:(h + 1) * DH], st[firsts[h], c % 2, :, h * DH:(h + 1) * DH], ACT.Copy)
                        e.inc(last, "st1_ready")
                        if c + 2 < CH:
                            blocks32(c + 2)
                        e.wait("nsq_ps", c)
                        for h in range(2):
                            for a, part in enumerate((firsts[h], seconds[h])):
                                col = (2 * h + a) * DH
                                last = fn(st2[part, :, col:col + DH], st[part, c % 2, :, h * DH:(h + 1) * DH], ACT.Square, scale=0.5 ** 0.5)
                        e.inc(last, "st2_ready")
                        if c + 1 < CH:
                            ahead2(c + 1)
                        e.wait("y_ps", c + 1)
                        e.inc(fn(kg[:, c, :, :], ps[6][:, 0:256].rearrange("p (b t) -> p b t", b=2), ACT.Copy), "y_ready")
                        if c + 1 < CH:
                            ahead3(c + 1)
                    e.wait("y_ready", CH)
                    for b in range(2):
                        e.inc(act.dma_start(dram["yT"][bass.ts(hp, P), bass.ds(bp * (2 * T) + b * T, T)].rearrange("p (c t) -> p c t", c=CH),
                                            kg[:, :, b, :]), "y_out", 16)

        @block.gpsimd
        def _(pool):
            g = nc.gpsimd
            g.memset(ident_bf[:], 0.0).then_inc(setup2, 1)
            g.memset(mask_bf[:], 0.0).then_inc(setup2, 1)
            g.memset(upto2[:], 1.0).then_inc(setup2, 1)
            g.memset(ones[:], 1.0).then_inc(setup, 1)
            for t in (st, st1, st2):
                g.memset(t[:], 0.0).then_inc(setup, 1)
            g.memset(ring[:], 0.0).then_inc(setup, 1)
            g.memset(m32[:], 0.0).then_inc(setup, 1)
            pool.wait_ge(setup2, 3)
            g.affine_select(out=ident_bf[:], in_=ident_bf[:], compare_op=ALU.not_equal, fill=1.0, base=0,
                            pattern=[[-1, P]], channel_multiplier=1).then_inc(setup, 1)
            g.affine_select(out=mask_bf[:], in_=mask_bf[:], compare_op=ALU.is_ge, fill=-1e30, base=0,
                            pattern=[[0, M4], [1, P]], channel_multiplier=-1).then_inc(setup, 1)
            g.affine_select(out=upto2[:], in_=upto2[:], compare_op=ALU.is_ge, fill=0.0, base=0,
                            pattern=[[1, P]], channel_multiplier=-1).then_inc(setup, 1)
            with units(nc.gpsimd) as hp:
                with nc.gpsimd.Fori(0, 2) as bp:
                    e = At(pool, hp * 2 + bp)
                    e.wait("vec_ready", 1)
                    vec = lambda t, c: t[:, of(c)].unsqueeze(2).broadcast_to([P, M4, DH])
                    by_m = lambda t: t.rearrange("p b (h j) -> p (b h) j", h=2)
                    e.wait("kv_tok", CH)
                    for c in range(CH):
                        mv = by_m(tok[:, c, 1, :, :])
                        e.inc(g.tensor_tensor(mv, mv, vec(root, c), ALU.mult), "mv_ready")
                    for c in range(CH):
                        e.wait("g_ready", c + 1)
                        if c == 0:
                            e.wait("w1_ps", 0)
                            e.wait("y_ps", 0)
                            e.wait("sg_ready", 0)
                            e.wait("y_out", 0)
                        g.tensor_tensor(kg[:, c, :, :], kc[:, c, :, :], gb[:, c % 2, :, :], ALU.mult)
                        g.tensor_copy(g_end[:, c, :], gb[:, c % 2, :, P - 1])
                        e.inc(g.tensor_tensor(qg[:, c, :, :], qc[:, c, :, :], gb[:, c % 2, :, :], ALU.mult), "kgqg_ready")

                    for c in range(CH):
                        e.wait("u_ready", c + 1)
                        e.inc(g.tensor_tensor(s2, u[:], vec(half_ss, c), ALU.mult), "norm_chain")
                        e.wait("t1_ready", c + 1)
                        e.wait("norm_chain", 4 * c + 1)
                        e.inc(g.tensor_tensor(s2, s2, t1[:], ALU.add), "norm_chain")
                        e.wait("norm_chain", 4 * c + 2)
                        e.inc(g.tensor_tensor(s2, s2, u[:], ALU.mult), "norm_chain")
                        e.wait("a1_ready", c + 1)
                        e.inc(g.tensor_tensor(inc[:, :, 0, :], u[:], a1[:], ALU.mult), "norm_chain")
                        e.wait("norm_chain", 4 * c + 4)
                        e.inc(g.tensor_tensor(inc[:, :, 1, :], s2, inc[:, :, 0, :], ALU.subtract), "inc_ready")

        @block.vector
        def _(dve):
            d = nc.vector
            dve.wait_ge(setup, 9)
            d.memset(xb[:], 0.0).then_inc(setup3, 1)
            dve.wait_ge(setup3, 1)
            d.memset(xb[:, 0, :, :].rearrange("p s t -> p (s t)")[:, 0:W * W:W + 1], 1.0).then_inc(setup3, 1)
            with units(nc.vector) as hp:
                with nc.vector.Fori(0, 2) as bp:
                    e = At(dve, hp * 2 + bp)
                    vec = lambda t, c: t[:, of(c)].unsqueeze(2).broadcast_to([P, M4, DH])
                    n = [0]

                    def link(ins):
                        n[0] += 1
                        e.inc(ins, "vec_chain")
                        e.wait("vec_chain", n[0])

                    e.wait("m_ready", 0)
                    e.wait("gam_ready", 0)
                    for dst, src in ((la, log_decay), (bt, beta), (ng, neg_cumlog)):
                        view = src[:].rearrange("p (b c) h -> p c b h", b=B)[:, :, bass.ds(bp * 2, 2), bass.ds(hp * 2, 2)]
                        last = d.tensor_copy(dst[:].rearrange("p (c b h) -> p c b h", c=CH, b=2), view)
                    link(last)
                    e.wait("h_ready", 0)
                    e.wait("out_added", 0)
                    d.tensor_copy(b1_now[:], b1[:, bass.ds(hp * KF, KF)])
                    e.inc(d.tensor_copy(wte_now[:], wte[:, bass.ds(bp * (GU * GT), GU * GT), bass.ds(hp, 1)].rearrange("p n o -> p (n o)")),
                          "moe_vecs")
                    for c in range(CH):
                        e.wait("k_sq", c + 1)
                        e.inc(d.tensor_reduce(ss[:, of(c), :].rearrange("p m a -> p (m a)"),
                                              sq[:, c % 2, :, :].rearrange("p b (x j) -> p (b x) j", j=32), AX.X, ALU.add), "ss_ready")
                    e.wait("ss_ready", CH)
                    link(d.tensor_tensor(root[:], ss[:, :, 0], ss[:, :, 1], ALU.add))
                    e.wait("norm_chain", 0)
                    link(d.tensor_scalar(half_ss[:], root[:], 0.5, None, ALU.mult))
                    link(d.tensor_scalar(half_ss1[:], ss[:, :, 0], 0.5, None, ALU.mult))
                    e.wait("root_ready", 1)
                    link(d.tensor_scalar(root[:], root[:], NORM_EPS, None, ALU.max))
                    link(d.reciprocal(inv_n2[:], root[:]))
                    link(d.tensor_tensor(c_m[:], inv_n2[:], bt[:], ALU.mult))
                    link(d.tensor_tensor(c_m[:], c_m[:], inv_n2[:], ALU.mult))
                    assert n[0] == PER["vec_chain"], n
                    e.inc(d.tensor_scalar(neg_c[:], c_m[:], -1.0, None, ALU.mult), "vec_ready")
                    for c in range(CH):
                        e.wait("kk_ps", c + 1)
                        e.wait("gam_ready", c + 1)
                        if c == 0:
                            e.wait("w64_ps", 0)
                            e.wait("m32_ready", 0)
                        for m in range(M4):
                            cm = c * M4 + m
                            last = d.scalar_tensor_tensor(out=neg_m[:, cm, :], in0=kk_ps[c % 2][m % 2][:, m // 2 * P:(m // 2 + 1) * P], scalar=neg_c[:, cm:cm + 1],
                                                          in1=gam[:, cm, :], op0=ALU.mult, op1=ALU.mult)
                        e.inc(last, "m_ready")
                    e.wait("diag_in", 16)
                    e.wait("inv_out", 0)
                    i = 0
                    for s in range(W - 2, -1, -1):
                        w = W - 1 - s
                        e.inc(d.tensor_tensor(prod[:, 0:w, 0:w], xb[:, 0, s + 1:W, s + 1:W].rearrange("p r t -> p t r"),
                                              diag[:, s:s + 1, s + 1:W].broadcast_to([P, w, w]), ALU.mult), "inv_chain")
                        i += 1
                        e.wait("inv_chain", i)
                        e.inc(d.tensor_reduce(xb[:, 0, s, s + 1:W], prod[:, 0:w, 0:w], AX.X, ALU.add), "inv_chain")
                        i += 1
                        e.wait("inv_chain", i)
                    e.inc(d.tensor_copy(xb[:, 1, :, :], xb[:, 0, :, :].rearrange("p s t -> p t s")), "inv_ready")

                    for g in range(GU):
                        e.wait("out_ps", g + 1)
                        for j in range(GT):
                            n = g * GT + j
                            row = res[:, bass.ds(bp * (GU * GT) + n, 1), :].rearrange("p o d -> p (o d)")
                            last = d.scalar_tensor_tensor(out=row, in0=ps[4 + g][:, j * P:(j + 1) * P], scalar=wte_now[:, n:n + 1],
                                                          in1=row, op0=ALU.mult, op1=ALU.add)
                        e.inc(last, "out_added")

                    def decays(c):
                        e.wait("kk1_ps", c + 1)
                        e.wait("y_ps", c - 1)
                        e.inc(d.tensor_tensor(by_bh(pT[:, c % 2, :, :]), pair(0), by_bh(gam[:, of(c), :]), ALU.mult), "p_ready")
                        e.wait("w1_ps", c - 1)
                        e.inc(d.tensor_tensor(by_bh(kg1[:, c % 2, :, :]), pair(1), by_bh(gam[:, of(c), :]), ALU.mult), "kg1_ready")

                    def inverse(c):
                        e.wait("x32_ps", c + 1)
                        e.wait("z_ps", c - 1)
                        e.inc(d.tensor_tensor(x2[:, c % 2, :, :], m4(1), ring[:, c % 2, 0, :, :], ALU.add), "x2_ready")
                        e.wait("t32_ps", c + 1)
                        e.wait("w64_ps", c)
                        e.inc(d.tensor_tensor(t2[:], ps[2][0:64, 0:256].rearrange("p (m t) -> p m t", m=M4),
                                              ring[0:64, c % 2, 1, :, 0:64], ALU.add), "t2_ready")

                    def norms(c):
                        e.wait("nsq_ps", c + 1)
                        e.inc(d.tensor_reduce(most[:, c:c + 1], ps[7][:], AX.X, ALU.max), "nmax_ready")

                    e.wait("end_check", 0)
                    e.inc(d.memset(st[:, 0, :, :], 0.0), "inv_chain")
                    e.wait("inv_chain", i + 1)
                    decays(0)
                    inverse(0)
                    lo = ps[5][:, 0:256].rearrange("p (m i) -> p m i", m=M4)
                    hi = ps[7][:, 0:256].rearrange("p (m i) -> p m i", m=M4)
                    for c in range(CH):
                        e.wait("z0_ps", c + 1)
                        e.wait("z_ps", c)
                        if c == 0:
                            e.wait("mv_ready", CH)
                            e.wait("kgqg_ready", CH)
                        mv = tok[:, c, 1, :, :].rearrange("p b (h j) -> p (b h) j", h=2)
                        e.inc(d.tensor_tensor(r[:], mv, lo, ALU.subtract), "r_ready")
                        e.wait("s_ready", c)
                        e.inc(d.tensor_tensor(st_g[:], st[:, c % 2, :, :], g_end[:, c, :].unsqueeze(2).broadcast_to([P, 2, P]), ALU.mult), "sg_ready")
                        if c:
                            norms(c - 1)
                        if c + 1 < CH:
                            decays(c + 1)
                        e.wait("z_ps", c + 1)
                        e.wait("w1_ps", c)
                        e.wait("inc_ready", c)
                        e.inc(d.tensor_tensor(u[:], lo, vec(c_m, c), ALU.mult), "u_ready")
                        e.wait("u_ready", c + 1)
                        e.wait("s_ps", c)
                        e.inc(d.tensor_tensor(uc[:], u[:], gam[:, of(c), P - 1:P].broadcast_to([P, M4, DH]), ALU.mult), "uc_ready")
                        e.inc(d.tensor_tensor(t1[:], mv, lo, ALU.subtract), "t1_ready")
                        e.inc(d.tensor_tensor(s1, u[:], vec(half_ss1, c), ALU.mult), "s1_ready")
                        if c + 1 < CH:
                            inverse(c + 1)
                        e.wait("s_ps", c + 1)
                        e.wait("sg_ready", c + 1)
                        e.wait("y_ps", c)
                        e.wait("w1_ps", c)
                        e.wait("st2_ready", c)
                        e.wait("st1_ready", c)
                        for h in range(2):
                            i_h = slice(h * DH, (h + 1) * DH)
                            last = d.tensor_tensor(st[heads[h], (c + 1) % 2, :, i_h], st_g[heads[h], :, i_h],
                                                   ps[6][heads[h], 256:384].rearrange("p (b i) -> p b i", b=2), ALU.add)
                        e.inc(last, "s_ready")
                        e.wait("s1_ready", c + 1)
                        e.wait("w1_ps", c + 1)
                        e.inc(d.tensor_tensor(a1[:], hi, s1, ALU.subtract), "a1_ready")
                    norms(CH - 1)
                    e.wait("nmax_ready", CH)
                    e.wait("s_ready", CH)
                    count = hp * 4 + bp * 2
                    d.tensor_scalar(scr[:, 0:CH], most[:], NORM_LIMIT, None, ALU.is_le, ALU.add, accum_out=bad[:, bass.ds(count, 1)])
                    e.inc(d.tensor_scalar(scr[:, CH:CH + 2 * P], st[:, 0, :, :].rearrange("p b i -> p (b i)"), CLIP, None, ALU.is_le, ALU.add,
                                    accum_out=bad[:, bass.ds(count + 1, 1)]), "end_check")
            dve.wait_ge(sems["end_check"], UNITS + 1)
            d.tensor_scalar(scr, neg_cumlog[:].rearrange("p n h -> p (n h)"), LOG_LIMIT, None, ALU.is_le, ALU.add,
                            accum_out=bad[:, UNITS * 2:UNITS * 2 + 1]).then_inc(setup2, 1)
            dve.wait_ge(setup2, 4)
            d.tensor_reduce(bad_sum[:], bad[:], AX.X, ALU.add).then_inc(fin, 1)
            dve.wait_ge(fin_ps, 1)
            good = P * (UNITS * (CH + 2 * P) + 512)
            d.tensor_scalar(unsafe[:], ps[0][:, 0:1], float(good) - 0.5, None, ALU.is_lt).then_inc(fin, 1)
            dve.wait_ge(fin, 2)


def replay(nc, ctx, dram, tag=""):
    HALF = DH // 2
    TB = 32
    NB = T // TB
    G = B * H
    with ExitStack() as c2:
        def sb(name, shape):
            return c2.enter_context(nc.sbuf_tensor(name + tag, shape, F32))
        sem = lambda name: ctx.enter_context(nc.semaphore(name + tag))
        ab = sb("ab_all", [P, 2, T])
        qk = sb("qk", [P, 2, 2, DH, TB])
        v = sb("vrow", [P, 2, HALF, TB])
        y = sb("yrow", [P, 2, HALF, TB])
        a_now, na_now, b_now = sb("a_now", [P, TB]), sb("na_now", [P, TB]), sb("b_now", [P, TB])
        sq = sb("sq", [P, DH, TB])
        norm = sb("norm", [P, TB])
        state = sb("state", [P, HALF, DH])
        prod = sb("prod", [P, HALF, DH])
        qprod = sb("qprod", [P, 2, HALF, DH])
        old = sb("old", [P, HALF])
        upd = sb("upd", [P, HALF])
        ab_in, norm_sq, norm_root = sem("ab_all_in"), sem("norm_sq"), sem("norm_root")
        blk_in = [sem(f"blk_in{i}") for i in range(2)]
        y_out = [sem(f"y_out{i}") for i in range(2)]
        y_ready, chain_s, state_ready, qprod_ready = sem("y_ready"), sem("step_chain"), sem("state_ready"), sem("qprod_ready")
        LOADS = 2 * B * 3
        block = c2.enter_context(nc.Block())
        rows = lambda half, b: slice(half * G + b * H, half * G + (b + 1) * H)

        @block.sync
        def _(sp):
            for half in range(2):
                for b in range(B):
                    for i in range(2):
                        sp.dma_start(ab[rows(half, b), i, :], dram["ab"][i * H:(i + 1) * H, b * T:(b + 1) * T]).then_inc(ab_in, 16)
            sp.sem_inc(y_ready, 2)
            with nc.sync.Fori(0, NB // 2) as it:
                for par in range(2):
                    sp.wait_ge(y_ready, it * 2 + par + 1)
                    for half in range(2):
                        for b in range(B):
                            tok = bass.ds(it * (2 * TB) + (b * T + par * TB), TB)
                            for i in range(2):
                                sp.dma_start(qk[rows(half, b), par, i, :, :],
                                             dram["qkv"][i, :, tok].rearrange("(h j) t -> h j t", h=H)).then_inc(blk_in[par], 16)
                            sp.dma_start(v[rows(half, b), par, :, :],
                                         dram["qkv"][2, :, tok].rearrange("(h g i) t -> g h i t", h=H, g=2)[half]).then_inc(blk_in[par], 16)

        @block.tensor
        def _(pe):
            pe.nop()

        @block.gpsimd
        def _(pool):
            with nc.gpsimd.Fori(0, NB // 2) as it:
                for t in range(2 * TB):
                    par, tt = divmod(t, TB)
                    pool.wait_ge(state_ready, it * (2 * TB) + t + 1)
                    nc.gpsimd.tensor_tensor(qprod[:, t % 2, :, :], state[:],
                                            qk[:, par, 0, :, tt:tt + 1].rearrange("p j o -> p o j").broadcast_to([P, HALF, DH]),
                                            ALU.mult).then_inc(qprod_ready, 1)

        @block.scalar
        def _(act):
            with nc.scalar.Fori(0, NB // 2) as it:
                for par in range(2):
                    act.wait_ge(norm_sq, it * 2 + par + 1)
                    nc.scalar.activation(norm[:], norm[:], ACT.Sqrt).then_inc(norm_root, 1)
                    act.wait_ge(y_ready, it * 2 + par + 1 + 2)
                    for half in range(2):
                        for b in range(B):
                            tok = bass.ds(it * (2 * TB) + (b * T + par * TB), TB)
                            act.dma_start(dram["yT"][:, tok].rearrange("(h g i) t -> g h i t", h=H, g=2)[half],
                                          y[rows(half, b), par, :, :]).then_inc(y_out[par], 16)
            for par in range(2):
                act.wait_ge(y_out[par], NB // 2 * 2 * B * 16 + 16)

        @block.vector
        def _(dve):
            PER = 2 * (7 + 5 * TB)
            dve.wait_ge(ab_in, 4 * B * 16)
            nc.vector.memset(state[:], 0.0).then_inc(chain_s, 1)
            dve.sem_inc(qprod_ready, 1)
            for par in range(2):
                dve.sem_inc(y_out[par], 16)
            with nc.vector.Fori(0, NB // 2) as it:
                chain = Tally(chain_s, base=it * PER + 1)
                for par in range(2):
                    dve.wait_ge(blk_in[par], it * (LOADS * 16) + LOADS * 16)
                    cols = bass.ds(it * (2 * TB) + par * TB, TB)
                    chain.on(nc.vector.tensor_copy(a_now[:], ab[:, 0, cols]))
                    chain.on(nc.vector.tensor_copy(b_now[:], ab[:, 1, cols]))
                    chain.wait(dve)
                    chain.on(nc.vector.tensor_scalar(na_now[:], a_now[:], -1.0, None, ALU.mult))
                    kk = qk[:, par, 1, :, :]
                    chain.on(nc.vector.tensor_tensor(sq[:], kk, kk, ALU.mult))
                    chain.wait(dve)
                    nc.vector.tensor_reduce(norm[:], sq[:].rearrange("p j t -> p t j"), AX.X, ALU.add).then_inc(norm_sq, 1)
                    dve.wait_ge(norm_root, it * 2 + par + 1)
                    chain.on(nc.vector.tensor_scalar(norm[:], norm[:], NORM_EPS, None, ALU.max))
                    chain.wait(dve)
                    chain.on(nc.vector.reciprocal(norm[:], norm[:]))
                    chain.wait(dve)
                    chain.on(nc.vector.tensor_tensor(kk, kk, norm[:].unsqueeze(1).broadcast_to([P, DH, TB]), ALU.mult))
                    chain.wait(dve)
                    dve.wait_ge(y_out[par], it * (2 * B * 16) + 16)
                    for tt in range(TB):
                        t = par * TB + tt
                        k_t = qk[:, par, 1, :, tt:tt + 1].rearrange("p j o -> p o j").broadcast_to([P, HALF, DH])
                        chain.on(nc.vector.tensor_tensor(prod[:], state[:], k_t, ALU.mult))
                        chain.wait(dve)
                        chain.on(nc.vector.tensor_reduce(old[:], prod[:], AX.X, ALU.add))
                        chain.wait(dve)
                        chain.on(nc.vector.scalar_tensor_tensor(out=upd[:], in0=old[:], scalar=na_now[:, tt:tt + 1],
                                                                in1=v[:, par, :, tt], op0=ALU.mult, op1=ALU.add))
                        chain.wait(dve)
                        chain.on(nc.vector.scalar_tensor_tensor(out=prod[:], in0=upd[:].unsqueeze(2).broadcast_to([P, HALF, DH]),
                                                                scalar=b_now[:, tt:tt + 1], in1=k_t, op0=ALU.mult, op1=ALU.mult))
                        chain.wait(dve)
                        dve.wait_ge(qprod_ready, it * (2 * TB) + t + 1)
                        chain.on(nc.vector.scalar_tensor_tensor(out=state[:], in0=state[:], scalar=a_now[:, tt:tt + 1],
                                                                in1=prod[:], op0=ALU.mult, op1=ALU.add))
                        chain.wait(dve)
                        nc.vector.tensor_scalar(state[:], state[:], CLIP, -CLIP, ALU.min, ALU.max).then_inc(state_ready, 1)
                        dve.wait_ge(state_ready, it * (2 * TB) + t + 1)
                        if tt >= 1:
                            dve.wait_ge(qprod_ready, it * (2 * TB) + t + 1)
                            nc.vector.tensor_reduce(y[:, par, :, tt - 1], qprod[:, (t - 1) % 2, :, :], AX.X, ALU.add)
                    dve.wait_ge(qprod_ready, it * (2 * TB) + (par + 1) * TB + 1)
                    nc.vector.tensor_reduce(y[:, par, :, TB - 1], qprod[:, (TB - 1) % 2, :, :], AX.X, ALU.add).then_inc(y_ready, 1)
                assert chain.n == PER, (chain.n, PER)


def gate_and_output(nc, ctx, ps, xT, res, dram, out):
    with ExitStack() as c2:
        def sb(name, shape):
            return c2.enter_context(nc.sbuf_tensor(name, shape, F32))
        sem = lambda name: ctx.enter_context(nc.semaphore(name))
        wg = sb("wg", [P, C])
        wo = sb("wo", [P, HP, D])
        bg = sb("bg", [P, HP])
        yt = sb("yt", [P, 2, HP, 512])
        gate = sb("gate", [P, 2, HP, 512])
        w_in, g_ps, g_ready = sem("wgo_in"), sem("g_ps"), sem("g_ready")
        y_in = [sem(f"y_in{i}") for i in range(2)]
        gated, o_ps, o_ready, o_out = sem("gated"), sem("o_ps"), sem("o_ready"), sem("o_out")
        block = c2.enter_context(nc.Block())
        out_tiles = out.rearrange("b (n p) d -> p (b n) d", p=P)

        @block.sync
        def _(sp):
            sp.dma_start(wg[:], dram["WgT"]).then_inc(w_in, 16)
            sp.dma_start(wo[:], dram["WoT"].rearrange("(h p) d -> p h d", p=P)).then_inc(w_in, 16)
            with nc.allow_non_contiguous_dma("bg is small"):
                sp.dma_start(bg[:], dram["bg"].rearrange("(h p) -> p h", p=P)).then_inc(w_in, 16)
            for g in range(NG):
                if g >= 2:
                    sp.wait_ge(gated, (g - 1) * HP)
                sp.dma_start(yt[:, g % 2, :, :], dram["yT"][:, g * 512:(g + 1) * 512].rearrange("(h p) t -> p h t", p=P)).then_inc(y_in[g % 2], 16)

        @block.gpsimd
        def _(pool):
            for g in range(NG):
                pool.wait_ge(o_ready, g + 1)
                pool.dma_start(out_tiles[:, g * GT:(g + 1) * GT, :], res[:, g * GT:(g + 1) * GT, :]).then_inc(o_out, 16)
            pool.wait_ge(o_out, 16 * NG)

        @block.tensor
        def _(pe):
            pe.wait_ge(w_in, 48)
            for g in range(NG + 1):
                if g < NG:
                    for hp in range(HP):
                        u = g * HP + hp
                        if u >= 4:
                            pe.wait_ge(g_ready, u - 3)
                        nc.tensor.matmul(ps[u % 4][:], wg[:, hp * P:(hp + 1) * P], xT[:, g * 512:(g + 1) * 512],
                                         start=True, stop=True).then_inc(g_ps, 1)
                if g >= 1:
                    o = g - 1
                    pe.wait_ge(gated, (o + 1) * HP)
                    if o >= 2:
                        pe.wait_ge(o_ready, o - 1)
                    for j in range(GT):
                        for hp in range(HP):
                            last = nc.tensor.matmul(ps[4 + o % 2][:, j * P:(j + 1) * P], gate[:, o % 2, hp, j * P:(j + 1) * P],
                                                    wo[:, hp, :], start=(hp == 0), stop=(hp == HP - 1))
                    last.then_inc(o_ps, 1)

        @block.scalar
        def _(act):
            act.wait_ge(w_in, 48)
            for g in range(NG):
                if g >= 2:
                    act.wait_ge(o_ps, g - 1)
                for hp in range(HP):
                    u = g * HP + hp
                    act.wait_ge(g_ps, u + 1)
                    nc.scalar.activation(gate[:, g % 2, hp, :], ps[u % 4][:], ACT.Silu, bias=bg[:, hp:hp + 1]).then_inc(g_ready, 1)

        @block.vector
        def _(dve):
            for g in range(NG):
                dve.wait_ge(y_in[g % 2], (g // 2 + 1) * 16)
                for hp in range(HP):
                    dve.wait_ge(g_ready, g * HP + hp + 1)
                    nc.vector.tensor_tensor(gate[:, g % 2, hp, :], gate[:, g % 2, hp, :], yt[:, g % 2, hp, :],
                                            ALU.mult).then_inc(gated, 1)
                dve.wait_ge(o_ps, g + 1)
                rows = res[:, g * GT:(g + 1) * GT, :]
                nc.vector.tensor_tensor(rows, rows, ps[4 + g % 2][:].rearrange("p (j d) -> p j d", d=D),
                                        ALU.add).then_inc(o_ready, 1)


def build(nc, x, dram, out):
    with ExitStack() as ctx:
        PS = ctx.enter_context(nc.psum_tensor("PS", [P, 8, 512], F32))
        ps = [PS[:, i, :] for i in range(8)]
        xT = ctx.enter_context(nc.sbuf_tensor("xT", [P, S], F32))
        res = ctx.enter_context(nc.sbuf_tensor("res", [P, NT, D], F32))
        wte = ctx.enter_context(nc.sbuf_tensor("wte", [P, NT, E], F32))
        ident = ctx.enter_context(nc.sbuf_tensor("ident", [P, P], F32))
        gates = [ctx.enter_context(nc.sbuf_tensor(name, [P, NT, H], F32)) for name in ("log_decay", "beta", "neg_cumlog")]
        unsafe = ctx.enter_context(nc.sbuf_tensor("unsafe", [P, 1], mybir.dt.int32))
        norm_and_route(nc, ctx, ps, x, xT, res, wte, ident, gates, dram)
        b1 = ctx.enter_context(nc.sbuf_tensor("b1", [P, E * KF], F32))
        expert_biases(nc, ctx, ps, res, wte, b1, ident, dram)
        project(nc, ctx, ps, xT, dram)
        chunked(nc, ctx, PS, ps, xT, res, wte, b1, ident, gates, unsafe, dram)
        if FALLBACK:
            flag = nc.values_load(unsafe[0:1, 0:1], min_val=0, max_val=1)
            with nc.If(flag != 0):
                replay(nc, ctx, dram)
        gate_and_output(nc, ctx, ps, xT, res, dram, out)


def kernel(**inputs):
    import numpy as np
    import concourse.bacc as bacc
    from concourse.bass_utils import run_bass_kernel_spmd

    attn = {k[len("L0_attn_"):]: v for k, v in inputs.items() if k.startswith("L0_attn_")}
    ffn = {k[len("L0_ffn_"):]: v for k, v in inputs.items() if k.startswith("L0_ffn_")}
    laid = {"x": attn["hidden_states"]}
    for name in ("Wq", "Wk", "Wv", "Wa", "Wb", "Wg", "Wo"):
        laid[name + "T"] = np.transpose(attn[name])
    for name in ("ba", "bb", "bg", "conv_q_w", "conv_q_b", "conv_k_w", "conv_k_b", "conv_v_w", "conv_v_b"):
        laid[name] = attn[name]
    laid.update(ffn)

    nc = bacc.Bacc("TRN2", target_bir_lowering=False, num_devices=1)
    arrays, dram = {}, {}
    for name, a in laid.items():
        a = np.ascontiguousarray(a)
        arrays["in_" + name] = a
        dram[name] = nc.dram_tensor("in_" + name, a.shape, mybir.dt.from_np(a.dtype), kind="ExternalInput").ap()
    out = nc.dram_tensor("out_0", (B, T, D), F32, kind="ExternalOutput").ap()
    dram["ab"] = nc.dram_tensor("ab_scratch", (2 * H, S), F32, kind="Internal").ap()
    dram["qkv"] = nc.dram_tensor("qkv_scratch", (3, C, S), F32, kind="Internal").ap()
    dram["yT"] = nc.dram_tensor("y_scratch", (C, S), F32, kind="Internal").ap()
    dram["diag"] = nc.dram_tensor("diag_scratch", (4, 8 * 4, 32 * 32), F32, kind="Internal").ap()
    dram["inverse"] = nc.dram_tensor("inverse_scratch", (4, 8, 2, 4, 32 * 32), F32, kind="Internal").ap()
    build(nc, dram["x"], dram, out)
    got = run_bass_kernel_spmd(nc, [arrays], core_ids=[0])
    return got.results[0]["out_0"]
```
